# Optimizing a Trainium2 kernel written in Bass

```python
import numpy as np
import jax
import jax.numpy as jnp

def _softmax(x, axis=-1):
    return jax.nn.softmax(x, axis=axis)

def _gelu(x):
    return jax.nn.gelu(x, approximate=True)

def _silu(x):
    return jax.nn.silu(x)

def _sigmoid(x):
    return jax.nn.sigmoid(x)

def _layernorm(x, axis=-1, eps=1e-05):
    m = jnp.mean(x, axis=axis, keepdims=True)
    v = jnp.var(x, axis=axis, keepdims=True)
    return (x - m) / jnp.sqrt(v + eps)

def _scatter_add(tgt, idx, src, axis=0):
    return tgt.at[idx].add(src)

def _segment_sum(src, seg, n):
    return jax.ops.segment_sum(src, seg, n)
kernel_name = 'mk_gnn_preln_d1_gnn_r8_f63f50'

def setup_inputs(seed: int=0):
    np.random.seed(seed)
    _w = jnp.asarray

    def _rec_inputs():
        import jax
        import jax.numpy as jnp
        _gk = jax.random.key(seed)
        x = -0.0005121 + 1.001 * jax.random.normal(jax.random.fold_in(_gk, 1), (12500, 64), jnp.float32)
        src = jax.random.randint(jax.random.fold_in(_gk, 2), (400000,), 0, 12500, jnp.int32)
        dst = jax.random.randint(jax.random.fold_in(_gk, 3), (400000,), 0, 12500, jnp.int32)
        _o = jnp.argsort(dst, stable=True)
        src = src[_o]
        dst = dst[_o]
        edge_attr_3 = 0.000669165 + 0.999965 * jax.random.normal(jax.random.fold_in(_gk, 11), (400000, 3), jnp.float32)
        return (x, src, dst, edge_attr_3)
    x, src, dst, edge_attr_3 = _rec_inputs()

    def _L0_gnn_setup():
        import jax, jax.numpy as jnp
        import numpy as np
        N, E = (6250, 100000)
        C, ED, L = (64, 3, 3)
        EPS = 1e-05

        def _layer_norm(h, g, b):
            mu = jnp.mean(h, axis=-1, keepdims=True)
            var = jnp.var(h, axis=-1, keepdims=True)
            return (h - mu) * jax.lax.rsqrt(var + EPS) * g + b
        key = jax.random.key(seed)
        ks = jax.random.split(key, 20)
        s = 0.1
        inp = {'x': jax.random.normal(ks[0], (N, C), dtype=jnp.float32), 'edge_index': jax.random.randint(ks[1], (2, E), 0, N, dtype=jnp.int64), 'edge_attr': jax.random.normal(ks[2], (E, ED), dtype=jnp.float32), 'W_node': jax.random.normal(ks[3], (L, C, C), dtype=jnp.float32) * s, 'W_e1': jax.random.normal(ks[4], (L, ED, C), dtype=jnp.float32) * s, 'b_e1': jnp.zeros((L, C), dtype=jnp.float32), 'W_e2': jax.random.normal(ks[5], (L, C, C), dtype=jnp.float32) * s, 'b_e2': jnp.zeros((L, C), dtype=jnp.float32), 'Wa1': jax.random.normal(ks[6], (L, 2 * C + ED, C), dtype=jnp.float32) * s, 'ba1': jnp.zeros((L, C), dtype=jnp.float32), 'Wa2': jax.random.normal(ks[7], (L, C, 1), dtype=jnp.float32) * s, 'ba2': jnp.zeros((L, 1), dtype=jnp.float32), 'bias': jnp.zeros((L, C), dtype=jnp.float32), 'ln_g': jnp.ones((L, C), dtype=jnp.float32), 'ln_b': jnp.zeros((L, C), dtype=jnp.float32)}
        return inp
    _L0_gnn_all = _L0_gnn_setup()
    _L0_gnn_in = {k: v for k, v in _L0_gnn_all.items() if k in ('W_node', 'W_e1', 'b_e1', 'W_e2', 'b_e2', 'Wa1', 'ba1', 'Wa2', 'ba2', 'bias', 'ln_g', 'ln_b')}
    del _L0_gnn_all
    return {'x': x, 'src': src, 'dst': dst, 'edge_attr_3': edge_attr_3, 'L0_gnn_W_node': _L0_gnn_in['W_node'], 'L0_gnn_W_e1': _L0_gnn_in['W_e1'], 'L0_gnn_b_e1': _L0_gnn_in['b_e1'], 'L0_gnn_W_e2': _L0_gnn_in['W_e2'], 'L0_gnn_b_e2': _L0_gnn_in['b_e2'], 'L0_gnn_Wa1': _L0_gnn_in['Wa1'], 'L0_gnn_ba1': _L0_gnn_in['ba1'], 'L0_gnn_Wa2': _L0_gnn_in['Wa2'], 'L0_gnn_ba2': _L0_gnn_in['ba2'], 'L0_gnn_bias': _L0_gnn_in['bias'], 'L0_gnn_ln_g': _L0_gnn_in['ln_g'], 'L0_gnn_ln_b': _L0_gnn_in['ln_b']}

def reference(x, src, dst, edge_attr_3, L0_gnn_W_node, L0_gnn_W_e1, L0_gnn_b_e1, L0_gnn_W_e2, L0_gnn_b_e2, L0_gnn_Wa1, L0_gnn_ba1, L0_gnn_Wa2, L0_gnn_ba2, L0_gnn_bias, L0_gnn_ln_g, L0_gnn_ln_b):
    import jax
    import jax.numpy as jnp

    def _L0_gnn_ref(x, edge_index, edge_attr, W_node, W_e1, b_e1, W_e2, b_e2, Wa1, ba1, Wa2, ba2, bias, ln_g, ln_b):
        import jax, jax.numpy as jnp
        import numpy as np
        N, E = (6250, 100000)
        C, ED, L = (64, 3, 3)
        EPS = 1e-05

        def _layer_norm(h, g, b):
            mu = jnp.mean(h, axis=-1, keepdims=True)
            var = jnp.var(h, axis=-1, keepdims=True)
            return (h - mu) * jax.lax.rsqrt(var + EPS) * g + b
        src = edge_index[0]
        dst = edge_index[1]
        n = x.shape[0]
        h = x
        for l in range(W_node.shape[0]):
            h_in = h
            hx = h @ W_node[l]
            ef = jax.nn.relu(edge_attr @ W_e1[l] + b_e1[l]) @ W_e2[l] + b_e2[l]
            xi = hx[dst]
            xj = hx[src]
            att_in = jnp.concatenate([xi, xj, edge_attr], axis=-1)
            a = jax.nn.sigmoid(jax.nn.relu(att_in @ Wa1[l] + ba1[l]) @ Wa2[l] + ba2[l])
            msg = a * (xj + ef)
            out = jax.ops.segment_sum(msg, dst, num_segments=n) + bias[l]
            out = _layer_norm(out, ln_g[l], ln_b[l])
            if l < W_node.shape[0] - 1:
                out = jax.nn.relu(out)
            h = out + h_in
        return h
    edge_index = jnp.stack([src, dst])
    h = jnp.maximum(_layernorm(x, axis=-1), 0.0)
    x = x + _L0_gnn_ref(h, edge_index, edge_attr_3, L0_gnn_W_node, L0_gnn_W_e1, L0_gnn_b_e1, L0_gnn_W_e2, L0_gnn_b_e2, L0_gnn_Wa1, L0_gnn_ba1, L0_gnn_Wa2, L0_gnn_ba2, L0_gnn_bias, L0_gnn_ln_g, L0_gnn_ln_b)
    return x

_drawn_inputs = setup_inputs


def setup_inputs(seed=0):
    import zlib

    import numpy as np

    out = dict(_drawn_inputs(seed))
    spreads = {'L0_gnn_b_e1': (0.0, 0.1),
     'L0_gnn_b_e2': (0.0, 0.1),
     'L0_gnn_ba1': (0.0, 0.8),
     'L0_gnn_ba2': (0.0, 0.8),
     'L0_gnn_bias': (0.0, 0.8),
     'L0_gnn_ln_g': (1.0, 0.2),
     'L0_gnn_ln_b': (0.0, 0.1)}
    factors = {'edge_attr_3': 3.251, 'L0_gnn_Wa1': 4.053, 'L0_gnn_Wa2': 4.747}
    for name, (base, spread) in spreads.items():
        noise = np.random.default_rng([zlib.crc32(name.encode()), seed]).standard_normal(out[name].shape)
        drawn = base * np.exp(spread * noise) if base else spread * noise
        out[name] = jnp.asarray(drawn.astype(out[name].dtype))
    for name, factor in factors.items():
        out[name] = (out[name] * factor).astype(out[name].dtype)
    return out
```

```python
from contextlib import ExitStack

import numpy as np

import concourse.bass as bass
from concourse import mybir

F32 = mybir.dt.float32
I32 = mybir.dt.int32
I16 = mybir.dt.int16
ALU = mybir.AluOpType
ACT = mybir.ActivationFunctionType
AX = mybir.AxisListType

P = 128
TILES = 5
EDGES = P * TILES
WIN = 32
WIN_BITS = 5
SLOTS = 4
AHEAD = SLOTS - 1
GB = 7
EPS = 1e-5
START = SLOTS
BEYOND_STEPS = 9


def gnn_kernel(nc, x, src_t, dst_t, dst, eattr_t, w_node, w_node_t, w_e1, b_e1, w_e2, b_e2,
               wa1, ba1, wa2, ba2, bias, ln_g, ln_b, ident, ones, out):
    N, C = x.shape
    L = w_node.shape[0]
    E = dst.shape[0]
    S = E // EDGES
    ROUNDS = S // SLOTS
    T = E // P
    BLOCKS = -(-N // P)
    GROUPS = BLOCKS // GB
    NPAD = BLOCKS * P
    FULL = N // P
    REST = N - FULL * P
    assert S * EDGES == E and S == ROUNDS * SLOTS + 1 and S % 5 == 0 and GROUPS * GB == BLOCKS
    assert GROUPS % 2 == 0 and REST > 0 and WIN == 1 << WIN_BITS
    SP_ROWS = S // 5
    COPIES = S + AHEAD
    CHUNK = GB * C

    ctx = ExitStack()
    with ctx:
        sb = lambda name, shape, dt=F32: ctx.enter_context(nc.sbuf_tensor(name, shape, dt))
        ps = lambda name, shape: ctx.enter_context(nc.psum_tensor(name, shape, F32))
        sem = lambda name: ctx.enter_context(nc.semaphore(name))
        dram = lambda name, shape, dt=F32: nc.dram_tensor(name, shape, dt, kind="Internal").ap()

        table = dram("gather_table", [NPAD, 2 * C])
        ptable = dram("p_table", [NPAD, C])
        rel_d = dram("dst_minus_base", [S, EDGES], I16)
        base_d = dram("base", [S])
        span_d = dram("span", [S])

        acc = sb("acc", [P, max(NPAD, 6400 + T)])
        h = sb("h", [P, BLOCKS, C])
        src_all = sb("src_all", [P, T + AHEAD * TILES], I32)
        rel_all = sb("rel_all", [P, T])
        base_i = sb("base_i", [1, S], I32)
        more_i = sb("more_i", [1, S], I32)
        first_i = sb("first_i", [1, S], I32)
        more_f = sb("more_f", [1, S])
        first_f = sb("first_f", [1, S])
        total_i = sb("total_i", [1, 1], I32)
        idn = sb("idn", [P, P])
        iota_w = sb("iota_w", [P, WIN])
        pidx = sb("pidx", [P, 1])
        eps_c = sb("eps_c", [P, 1])
        wn = sb("wn", [C + 1, 3 * C])
        wnt = sb("wnt", [C, C])
        wab = sb("wab", [C, 2 * C])
        we = sb("we", [4, 2 * C])
        wo = sb("wo", [P, C])
        wa2_b = sb("wa2_b", [P, C])
        ba2_b = sb("ba2_b", [P, 1])
        bias_b = sb("bias_b", [P, C])
        g_b = sb("g_b", [P, C])
        b_b = sb("b_b", [P, C])
        floor = sb("floor", [P, L])
        idx = sb("idx", [P, SLOTS, TILES], I32)
        msg = [sb(f"msg{k}", [P, TILES, 3 * C]) for k in range(SLOTS)]
        ea = [sb(f"ea{k}", [4, EDGES]) for k in range(SLOTS)]
        rel = [sb(f"rel{k}", [WIN, EDGES], I16) for k in range(SLOTS)]
        pwin = [sb(f"pwin{k}", [WIN, C]) for k in range(SLOTS)]
        pick = sb("pick", [WIN, 2, EDGES])
        z = sb("z", [P, TILES, C])
        zw = sb("zw", [P, TILES, C])
        logit = sb("logit", [P, 2, TILES])
        a = sb("a", [P, 2, TILES])
        hot = sb("hot", [P, TILES, WIN])
        ahot = sb("ahot", [P, 2, TILES, WIN])
        woff = sb("woff", [P, 1])
        drel = sb("drel", [P, TILES])
        hs = sb("hs", [P, 2, GB, C])
        hT = sb("hT", [C + 1, 2, GB * P])
        tabs = sb("tabs", [P, 2, GB, 3 * C])
        accs = sb("accs", [P, 2, GB * P])
        o1 = sb("o1", [P, GB, C])
        o2 = sb("o2", [P, GB, C])
        st = sb("st", [P, 4, GB])

        zr_ps = ps("zr_ps", [P, 4, 512])
        out_ps = ps("out_ps", [P, 2, 512])
        upd_ps = ps("upd_ps", [P, 2, 512])

        s_in = sem("inputs_landed")
        s_x = sem("x_landed")
        s_const = sem("constants_made")
        s_fl = sem("flat_dst_step")
        s_base_w = sem("base_written")
        s_base_r = sem("base_read")
        s_prep = sem("dst_tables_ready")
        s_ln0 = sem("first_ln_step")
        s_ln0v = sem("first_variance_ready")
        s_ln0r = sem("first_root_ready")
        s_h = sem("h_ready")
        s_w = sem("weights_landed")
        s_comp = sem("composite_product_ready")
        s_wn = sem("composite_weights_ready")
        s_zero = sem("acc_zeroed")
        s_hs = sem("h_staged")
        s_tr = sem("h_transposed")
        s_ht = sem("hT_ready")
        s_tab = sem("table_product_ready")
        s_tabs = sem("table_staged")
        s_tw = [sem(f"table_written{u}") for u in range(2)]
        s_idx = sem("indices_laid_out")
        s_mark = sem("waits_passed")
        s_gat = [sem(f"gathered{k}") for k in range(SLOTS)]
        s_ld = [sem(f"edge_loads_landed{k}") for k in range(SLOTS)]
        s_pick = sem("pick_ready")
        s_zr = sem("zr_ready")
        s_zsum = sem("z_summed")
        s_zw = sem("z_weighted")
        s_log = sem("logit_ready")
        s_r = sem("r_ready")
        s_a = sem("a_ready")
        s_hot = sem("hot_ready")
        s_ahot = sem("ahot_ready")
        s_sc = sem("messages_summed")
        s_acc = sem("acc_added")
        s_bd = sem("beyond_loads_landed")
        s_bg = sem("beyond_gathered")
        s_bs = sem("beyond_step")
        s_bi = sem("beyond_vector_step")
        s_as = sem("acc_staged")
        s_up = sem("update_product_ready")
        s_us = sem("update_step")
        s_var = sem("variance_ready")
        s_root = sem("root_ready")
        s_xf = sem("x_reloaded")
        s_fin = sem("output_ready")
        s_out = sem("output_written")

        block = ctx.enter_context(nc.Block())
        W_DMAS = 16 * 15
        VSTEPS = 7
        LSTEPS = 5

        def done(l, s):
            return l * S + s + (START + 1)

        def freed(l, s, ring):
            return l * S + s + (START + 1 - ring)

        def uses(l, i, k):
            return l * (ROUNDS + (k == 0)) + i

        def mark(eng):
            eng.sem_inc(s_mark, 1)

        def supertiles(eng, body):
            with eng.Fori(0, ROUNDS) as i:
                for k in range(SLOTS):
                    body(i, i * SLOTS + k, k)
            body(ROUNDS, ROUNDS * SLOTS, 0)

        def beyond(eng, l, body):
            mark(eng)
            total = eng.value_load(total_i[0:1, 0:1], min_val=0, max_val=S * BLOCKS * (P // WIN))
            with eng.If(total > 0):
                with eng.Fori(0, S) as s:
                    more = eng.value_load(more_i[0:1, bass.ds(s, 1)], min_val=0, max_val=BLOCKS * (P // WIN))
                    with eng.If(more > 0):
                        first = eng.value_load(first_i[0:1, bass.ds(s, 1)], min_val=0,
                                               max_val=S * BLOCKS * (P // WIN))
                        with eng.Fori(0, more) as v:
                            body(s, v, l * total + first + v)
                        eng.nop()
                    eng.nop()
                eng.nop()
            eng.nop()

        def tab_view():
            return zr_ps[:, :, :].rearrange("p b (u f) -> p (b u) f", u=2)

        def z_part(par): return zr_ps[:, 2 * par, 0:TILES * C].rearrange("p (j c) -> p j c", c=C)
        def r_part(par): return zr_ps[:, 2 * par + 1, 0:TILES * C].rearrange("p (j c) -> p j c", c=C)

        def dst_flat(): return acc[0:SP_ROWS, 0:5 * EDGES].bitcast(I32)
        def st_rel(): return acc[0:SP_ROWS, 3200:3200 + 5 * EDGES // 2].bitcast(I16)
        def st_base(): return acc[0:SP_ROWS, 4800:4805]
        def st_top(): return acc[0:SP_ROWS, 4808:4813]
        def st_span(): return acc[0:SP_ROWS, 4816:4821]
        def base_all(): return acc[:, 5000:5000 + S]
        def dst_cols(): return acc[:, 6400:6400 + T].bitcast(I32)
        def x_again(): return acc[:, 0:BLOCKS * C].rearrange("p (b c) -> p b c", c=C)

        @block.sync
        def _(sp):
            sp.dma_start(src_all[:, 0:T], src_t).then_inc(s_in, 16)
            sp.dma_start(acc[:, 6400:6400 + T].bitcast(I32), dst_t).then_inc(s_in, 16)
            sp.dma_start(acc[0:SP_ROWS, 0:5 * EDGES].bitcast(I32), dst.rearrange("(p n) -> p n", p=SP_ROWS)).then_inc(s_in, 16)
            sp.dma_start(idn[:, :], ident).then_inc(s_in, 16)
            sp.dma_start(hT[C:C + 1, 0, :], ones[0:1, 0:GB * P]).then_inc(s_in, 16)
            sp.dma_start(hT[C:C + 1, 1, :], ones[0:1, 0:GB * P]).then_inc(s_in, 16)
            for k in range(SLOTS):
                sp.dma_start(ea[k][0:1, :], ones[0:1, 0:EDGES]).then_inc(s_in, 16)
            sp.wait_ge(s_const, 1)
            sp.dma_start(h[:, 0:FULL, :], x[0:FULL * P, :].rearrange("(b p) c -> p b c", p=P)).then_inc(s_x, 16)
            sp.dma_start(h[0:REST, FULL, :], x[FULL * P:N, :]).then_inc(s_x, 16)
            sp.wait_ge(s_fl, 4)
            sp.dma_start(base_d.rearrange("(p n) -> p n", p=SP_ROWS), st_base()).then_inc(s_base_w, 16)
            sp.dma_start(span_d.rearrange("(p n) -> p n", p=SP_ROWS), st_span()).then_inc(s_base_w, 16)
            sp.dma_start(rel_d.rearrange("(p a) n -> p (a n)", p=SP_ROWS), st_rel()).then_inc(s_base_w, 16)
            sp.wait_ge(s_base_w, 48)
            sp.dma_start(base_all(), base_d.partition_broadcast(P)).then_inc(s_base_r, 16)
            sp.dma_start(more_f[0:1, :], span_d.rearrange("(a n) -> a n", a=1)).then_inc(s_base_r, 16)
            with sp.Fori(0, L) as l:
                sp.wait_ge(s_h, l + 1)
                row = lambda t: t[bass.ds(l, 1)]
                flat = lambda t: t[bass.ds(l, 1)].rearrange("a b c -> (a b) c")
                for dst_ap, src_ap in [
                        (wn[0:C, C:2 * C], flat(w_node)), (wnt[:, :], flat(w_node_t)),
                        (wn[C:C + 1, 0:C], row(ba1)), (wn[C:C + 1, C:2 * C], row(b_e2)),
                        (wab[:, C:2 * C], flat(wa1[:, 0:C])), (wab[:, 0:C], flat(wa1[:, C:2 * C])),
                        (we[1:4, 0:C], flat(wa1[:, 2 * C:2 * C + 3])), (we[1:4, C:2 * C], flat(w_e1)),
                        (we[0:1, C:2 * C], row(b_e1)), (wo[C:2 * C, :], flat(w_e2)),
                        (wa2_b[:, :], row(wa2.rearrange("l c a -> l (c a)")).to_broadcast([P, C])),
                        (ba2_b[:, :], row(ba2).to_broadcast([P, 1])),
                        (bias_b[:, :], row(bias).to_broadcast([P, C])),
                        (g_b[:, :], row(ln_g).to_broadcast([P, C])),
                        (b_b[:, :], row(ln_b).to_broadcast([P, C]))]:
                    sp.dma_start(dst_ap, src_ap).then_inc(s_w, 16)
                with sp.Fori(0, GROUPS // 2) as q2:
                    for u in range(2):
                        q = q2 * 2 + u
                        sp.wait_ge(s_tabs, l * GROUPS + q + 1)
                        rows = lambda t: t[bass.ds(q * (GB * P), GB * P), :].rearrange("(b p) f -> p b f", p=P)
                        sp.dma_start(rows(table), tabs[:, u, :, 0:2 * C]).then_inc(s_tw[u], 16)
                        sp.dma_start(rows(ptable), tabs[:, u, :, 2 * C:3 * C]).then_inc(s_tw[u], 16)
                for u in range(2):
                    sp.wait_ge(s_tw[u], (l + 1) * (GROUPS * 16))
                mark(sp)

                def loads(s, k, p_row, landed):
                    sp.dma_start(ea[k][1:4, :], eattr_t[:, bass.ds(s * EDGES, EDGES)]).then_inc(landed, 16)
                    sp.dma_start(rel[k][:, :], rel_d[bass.ds(s, 1), :].to_broadcast([WIN, EDGES])).then_inc(landed, 16)
                    sp.dma_start(pwin[k][:, :], ptable[bass.ds(p_row, WIN), :]).then_inc(landed, 16)

                def step(i, s, k):
                    base = sp.value_load(base_i[0:1, bass.ds(s, 1)], min_val=0, max_val=N - 1)
                    sp.wait_ge(s_zr, freed(l, s, SLOTS))
                    loads(s, k, base, s_ld[k])
                supertiles(sp, step)

                def window(s, v, c):
                    base = sp.value_load(base_i[0:1, bass.ds(s, 1)], min_val=0, max_val=N - 1)
                    sp.wait_ge(s_bs, c * BEYOND_STEPS)
                    row_ = nc.s_assert_within(base + v * WIN + WIN, 0, N - 1)
                    loads(s, 0, row_, s_bd)
                sp.wait_ge(s_acc, done(l, S - 1))
                beyond(sp, l, window)
            sp.wait_ge(s_h, L + 1)
            sp.dma_start(x_again()[:, 0:FULL, :], x[0:FULL * P, :].rearrange("(b p) c -> p b c", p=P)).then_inc(s_xf, 16)
            sp.dma_start(x_again()[0:REST, FULL, :], x[FULL * P:N, :]).then_inc(s_xf, 16)
            sp.wait_ge(s_fin, 2)
            sp.dma_start(out[0:FULL * P, :].rearrange("(b p) c -> p b c", p=P), h[:, 0:FULL, :]).then_inc(s_out, 16)
            sp.dma_start(out[FULL * P:N, :], h[0:REST, FULL, :]).then_inc(s_out, 16)
            sp.wait_ge(s_out, 32)

        @block.gpsimd
        def _(pool):
            pool.memset(h[:, FULL, :], 0.0).then_inc(s_const, 1)
            pool.memset(src_all[:, T:], 0)
            pool.memset(wn[:, :], 0.0)
            pool.memset(we[:, :], 0.0)
            pool.memset(eps_c[:, :], EPS)
            for l in range(L):
                pool.memset(floor[:, l:l + 1], 0.0 if l < L - 1 else -3.0e38)
            pool.iota(iota_w[:, :], pattern=[[1, WIN]], base=0, channel_multiplier=0,
                      allow_small_or_imprecise_dtypes=True)
            pool.iota(pidx[:, :], pattern=[[0, 1]], base=0, channel_multiplier=1,
                      allow_small_or_imprecise_dtypes=True).then_inc(s_const, 1)
            with pool.Fori(0, L) as l:
                pool.wait_ge(s_h, l + 1)
                mark(pool)
                pool.memset(acc[:, :], 0.0).then_inc(s_zero, 1)
                for u in range(2):
                    pool.wait_ge(s_tw[u], (l + 1) * (GROUPS * 16))
                mark(pool)

                def gather(k, landed):
                    for j in range(TILES):
                        pool.indirect_dma_start(
                            out=msg[k][:, j, 0:2 * C], out_offset=None, in_=table,
                            in_offset=bass.IndirectOffsetOnAxis(ap=idx[:, k, j:j + 1], axis=0)).then_inc(landed, 16)

                def step(i, s, k):
                    pool.wait_ge(s_idx, l * COPIES + s + 1)
                    pool.wait_ge(s_sc, freed(l, s, SLOTS))
                    mark(pool)
                    gather(k, s_gat[k])
                supertiles(pool, step)

                def window(s, v, c):
                    pool.wait_ge(s_bs, c * BEYOND_STEPS + 1)
                    mark(pool)
                    gather(0, s_bg)
                beyond(pool, l, window)

        @block.scalar
        def _(act):
            with act.Fori(0, GROUPS) as q:
                act.wait_ge(s_ln0v, q + 1)
                act.activation(st[:, 2, :], st[:, 1, :], ACT.Sqrt, bias=eps_c[:, :], scale=1.0 / C).then_inc(s_ln0r, 1)
            act.sem_inc(s_r, START)
            act.sem_inc(s_a, START)
            with act.Fori(0, L) as l:
                act.wait_ge(s_h, l + 1)
                with act.Fori(0, GROUPS // 2) as q2:
                    for u in range(2):
                        q = q2 * 2 + u
                        act.copy(hs[:, u, :, :], h[:, bass.ds(q * GB, GB), :]).then_inc(s_hs, 1)
                        act.wait_ge(s_tr, l * GROUPS + q + 1)
                        act.copy(hT[0:C, u, 0:512], out_ps[0:C, 0, :])
                        act.copy(hT[0:C, u, 512:GB * P], out_ps[0:C, 1, 0:GB * P - 512]).then_inc(s_ht, 1)

                def lay_out(i, s, k):
                    act.wait_ge(s_gat[k], uses(l, i, k) * (16 * TILES))
                    act.copy(idx[:, k, :], src_all[:, bass.ds(s * TILES, TILES)]).then_inc(s_idx, 1)
                for k in range(AHEAD):
                    lay_out(0, k, k)

                def relu_r(par, k):
                    act.activation(msg[k][:, :, 2 * C:3 * C], r_part(par), ACT.Relu).then_inc(s_r, 1)

                def step(i, s, k):
                    act.wait_ge(s_zr, done(l, s))
                    act.wait_ge(s_sc, freed(l, s, SLOTS))
                    relu_r(k % 2, k)
                    act.wait_ge(s_log, done(l, s))
                    act.wait_ge(s_ahot, freed(l, s, 2))
                    act.activation(a[:, k % 2, :], logit[:, k % 2, :], ACT.Sigmoid, bias=ba2_b[:, :]).then_inc(s_a, 1)
                    n = k + AHEAD
                    lay_out(i + n // SLOTS, s + AHEAD, n % SLOTS)
                supertiles(act, step)

                def window(s, v, c):
                    act.wait_ge(s_bs, c * BEYOND_STEPS)
                    act.copy(idx[:, 0, :], src_all[:, bass.ds(s * TILES, TILES)]).then_inc(s_bs, 1)
                    act.wait_ge(s_bs, c * BEYOND_STEPS + 3)
                    act.activation(msg[0][:, :, 2 * C:3 * C], r_part(0), ACT.Relu).then_inc(s_bs, 1)
                    act.wait_ge(s_bs, c * BEYOND_STEPS + 5)
                    act.activation(a[:, 0, :], logit[:, 0, :], ACT.Sigmoid, bias=ba2_b[:, :]).then_inc(s_bs, 1)
                act.wait_ge(s_acc, done(l, S - 1))
                beyond(act, l, window)
                act.wait_ge(s_bi, l + 1)
                with act.Fori(0, GROUPS // 2) as q2:
                    for u in range(2):
                        q = q2 * 2 + u
                        act.copy(accs[:, u, :], acc[:, bass.ds(q * (GB * P), GB * P)]).then_inc(s_as, 1)
                        act.wait_ge(s_var, l * GROUPS + q + 1)
                        act.activation(st[:, 2, :], st[:, 1, :], ACT.Sqrt, bias=eps_c[:, :], scale=1.0 / C).then_inc(s_root, 1)

        @block.tensor
        def _(pe):
            pe.sem_inc(s_zr, START)
            pe.sem_inc(s_sc, START)
            pe.wait_ge(s_in, 16 * (6 + SLOTS))
            with pe.Fori(0, L) as l:
                pe.wait_ge(s_w, (l + 1) * W_DMAS)
                mark(pe)
                pe.matmul(upd_ps[0:C, 0, 0:2 * C], wnt[:, :], wab[:, :], start=True, stop=True).then_inc(s_comp, 1)
                pe.wait_ge(s_wn, l + 1)
                mark(pe)
                with pe.Fori(0, GROUPS // 2) as q2:
                    for u in range(2):
                        q = q2 * 2 + u
                        pe.wait_ge(s_hs, l * GROUPS + q + 1)
                        mark(pe)
                        for j in range(GB):
                            t = pe.transpose(out_ps[0:C, j // 4, (j % 4) * P:(j % 4 + 1) * P], hs[:, u, j, :], idn[:, :])
                        t.then_inc(s_tr, 1)
                        pe.wait_ge(s_ht, l * GROUPS + q + 1)
                        pe.wait_ge(s_tabs, l * GROUPS + q)
                        for j in range(GB):
                            t = pe.matmul(tab_view()[:, j, 0:3 * C], hT[:, u, j * P:(j + 1) * P], wn[:, :],
                                          start=True, stop=True)
                        t.then_inc(s_tab, 1)
                pe.wait_ge(s_tabs, (l + 1) * GROUPS)

                def zr_product(par, k):
                    for j in range(TILES):
                        cols = slice(j * P, (j + 1) * P)
                        pe.matmul(z_part(par)[:, j, :], ea[k][:, cols], we[:, 0:C], start=True, stop=False)
                        pe.matmul(z_part(par)[:, j, :], pick[:, par, cols], pwin[k][:, :], start=False, stop=True)
                        t = pe.matmul(r_part(par)[:, j, :], ea[k][:, cols], we[:, C:2 * C], start=True, stop=True)
                    return t

                def message_sum(par, k):
                    for j in range(TILES):
                        t = pe.matmul(out_ps[:, par, 0:WIN], msg[k][:, j, C:3 * C], ahot[:, par, j, :],
                                      start=(j == 0), stop=(j == TILES - 1))
                    return t

                def sums(s, k):
                    pe.wait_ge(s_ahot, done(l, s))
                    pe.wait_ge(s_r, done(l, s))
                    pe.wait_ge(s_acc, freed(l, s, 2))
                    message_sum(k % 2, k).then_inc(s_sc, 1)

                def step(i, s, k, before):
                    pe.wait_ge(s_ld[k], (uses(l, i, k) + 1) * 48)
                    pe.wait_ge(s_pick, done(l, s))
                    pe.wait_ge(s_zsum, freed(l, s, 2))
                    pe.wait_ge(s_r, freed(l, s, 2))
                    zr_product(k % 2, k).then_inc(s_zr, 1)
                    if before:
                        sums(s - 1, (k - 1) % SLOTS)

                for k in range(SLOTS):
                    step(0, k, k, k > 0)
                with pe.Fori(1, ROUNDS) as i:
                    for k in range(SLOTS):
                        step(i, i * SLOTS + k, k, True)
                step(ROUNDS, ROUNDS * SLOTS, 0, True)
                sums(S - 1, 0)

                def window(s, v, c):
                    pe.wait_ge(s_bs, c * BEYOND_STEPS + 2)
                    zr_product(0, 0).then_inc(s_bs, 1)
                    pe.wait_ge(s_bs, c * BEYOND_STEPS + 7)
                    message_sum(0, 0).then_inc(s_bs, 1)
                pe.wait_ge(s_acc, done(l, S - 1))
                beyond(pe, l, window)
                with pe.Fori(0, GROUPS // 2) as q2:
                    for u in range(2):
                        q = q2 * 2 + u
                        pe.wait_ge(s_as, l * GROUPS + q + 1)
                        for j in range(GB):
                            t = pe.matmul(upd_ps[:, u, j * C:(j + 1) * C], accs[:, u, j * P:(j + 1) * P], wo[:, :],
                                          start=True, stop=True)
                        t.then_inc(s_up, 1)

        @block.vector
        def _(dve):
            f3 = dst_flat().rearrange("p (a n) -> p a n", n=EDGES)
            dve.wait_ge(s_in, 16 * (6 + SLOTS))
            dve.tensor_reduce(st_base(), f3, axis=AX.X, op=ALU.min).then_inc(s_fl, 1)
            dve.tensor_reduce(st_top(), f3, axis=AX.X, op=ALU.max).then_inc(s_fl, 1)
            dve.wait_ge(s_fl, 2)
            dve.tensor_tensor(st_span(), st_top(), st_base(), ALU.subtract).then_inc(s_fl, 1)
            dve.tensor_tensor(st_rel().rearrange("p (a n) -> p a n", n=EDGES), f3,
                              st_base().unsqueeze(2).to_broadcast([SP_ROWS, 5, EDGES]), ALU.subtract).then_inc(s_fl, 1)
            dve.tensor_copy(wo[0:C, :], idn[0:C, 0:C]).then_inc(s_prep, 1)
            dve.wait_ge(s_base_r, 32)
            dve.tensor_tensor(rel_all[:, :].rearrange("p (s j) -> p s j", j=TILES),
                              dst_cols().rearrange("p (s j) -> p s j", j=TILES),
                              base_all().unsqueeze(2).to_broadcast([P, S, TILES]), ALU.subtract).then_inc(s_prep, 1)
            dve.tensor_copy(base_i[0:1, :], base_all()[0:1, :]).then_inc(s_prep, 1)
            dve.tensor_copy(more_i[0:1, :], more_f[0:1, :]).then_inc(s_prep, 1)
            dve.wait_ge(s_prep, 4)
            dve.tensor_scalar(first_i[0:1, :], more_i[0:1, :], WIN_BITS, None, ALU.arith_shift_right).then_inc(s_prep, 1)
            dve.wait_ge(s_prep, 5)
            dve.tensor_copy(more_i[0:1, :], first_i[0:1, :]).then_inc(s_prep, 1)
            dve.tensor_copy(more_f[0:1, :], first_i[0:1, :]).then_inc(s_prep, 1)
            dve.wait_ge(s_prep, 7)
            dve.tensor_tensor_scan(first_f[0:1, :], more_f[0:1, :], more_f[0:1, :], 0.0, ALU.add, ALU.bypass).then_inc(s_prep, 1)
            dve.wait_ge(s_prep, 8)
            dve.tensor_copy(total_i[0:1, :], first_f[0:1, S - 1:S]).then_inc(s_prep, 1)
            dve.tensor_tensor(first_i[0:1, :], first_f[0:1, :], more_f[0:1, :], ALU.subtract).then_inc(s_prep, 1)

            dve.wait_ge(s_x, 32)
            dve.wait_ge(s_const, 2)

            def centred(n, chain, total):
                dve.tensor_reduce(st[:, 0, :], o1[:, :, :], axis=AX.X, op=ALU.add).then_inc(chain, 1)
                dve.wait_ge(chain, total + 1)
                dve.scalar_tensor_tensor(o2[:, :, :], st[:, 0, :].unsqueeze(2).to_broadcast([P, GB, C]), -1.0 / C,
                                         o1[:, :, :], ALU.mult, ALU.add).then_inc(chain, 1)
                dve.wait_ge(chain, total + 2)
                dve.tensor_tensor(o1[:, :, :], o2[:, :, :], o2[:, :, :], ALU.mult).then_inc(chain, 1)
                dve.wait_ge(chain, total + 3)

            with dve.Fori(0, GROUPS) as q:
                n = q * (LSTEPS + 1)
                grp = h[:, bass.ds(q * GB, GB), :]
                dve.wait_ge(s_ln0, n)
                dve.tensor_copy(o1[:, :, :], grp).then_inc(s_ln0, 1)
                dve.wait_ge(s_ln0, n + 1)
                centred(q, s_ln0, n + 1)
                dve.tensor_reduce(st[:, 1, :], o1[:, :, :], axis=AX.X, op=ALU.add).then_inc(s_ln0v, 1)
                dve.wait_ge(s_ln0r, q + 1)
                dve.reciprocal(st[:, 3, :], st[:, 2, :]).then_inc(s_ln0, 1)
                dve.wait_ge(s_ln0, n + 5)
                dve.scalar_tensor_tensor(grp, o2[:, :, :], 0.0, st[:, 3, :].unsqueeze(2).to_broadcast([P, GB, C]),
                                         ALU.max, ALU.mult).then_inc(s_ln0, 1)
            dve.wait_ge(s_ln0, GROUPS * (LSTEPS + 1))
            dve.wait_ge(s_prep, 10)
            dve.sem_inc(s_h, 1)
            for s_ in (s_pick, s_zsum, s_zw, s_log, s_hot, s_ahot, s_acc):
                dve.sem_inc(s_, START)

            with dve.Fori(0, L) as l:
                dve.wait_ge(s_comp, l + 1)
                dve.tensor_copy(wn[0:C, 0:C], upd_ps[0:C, 0, 0:C])
                dve.tensor_copy(wn[0:C, 2 * C:3 * C], upd_ps[0:C, 0, C:2 * C]).then_inc(s_wn, 1)
                with dve.Fori(0, GROUPS // 2) as q2:
                    for u in range(2):
                        q = q2 * 2 + u
                        dve.wait_ge(s_tab, l * GROUPS + q + 1)
                        dve.wait_ge(s_tw[u], (l * (GROUPS // 2) + q2) * 32)
                        dve.tensor_copy(tabs[:, u, :, :], tab_view()[:, 0:GB, 0:3 * C]).then_inc(s_tabs, 1)
                dve.wait_ge(s_zero, l + 1)

                def step(i, s, k):
                    par = k % 2
                    dve.wait_ge(s_ld[k], (uses(l, i, k) + 1) * 48)
                    dve.wait_ge(s_zr, freed(l, s, 2))
                    dve.tensor_scalar(pick[:, par, :], rel[k][:, :], pidx[0:WIN, :], None, ALU.is_equal).then_inc(s_pick, 1)
                    dve.wait_ge(s_ahot, freed(l, s, 1))
                    dve.tensor_tensor(hot[:, :, :], iota_w[:, :].unsqueeze(1).to_broadcast([P, TILES, WIN]),
                                      rel_all[:, bass.ds(s * TILES, TILES)].unsqueeze(2).to_broadcast([P, TILES, WIN]),
                                      ALU.is_equal).then_inc(s_hot, 1)
                    dve.wait_ge(s_zr, done(l, s))
                    dve.wait_ge(s_gat[k], (uses(l, i, k) + 1) * (16 * TILES))
                    dve.wait_ge(s_zw, freed(l, s, 1))
                    dve.tensor_tensor(z[:, :, :], z_part(par), msg[k][:, :, 0:C], ALU.add).then_inc(s_zsum, 1)
                    dve.wait_ge(s_zsum, done(l, s))
                    dve.wait_ge(s_log, freed(l, s, 1))
                    dve.scalar_tensor_tensor(zw[:, :, :], z[:, :, :], 0.0,
                                             wa2_b[:, :].unsqueeze(1).to_broadcast([P, TILES, C]),
                                             ALU.max, ALU.mult).then_inc(s_zw, 1)
                    dve.wait_ge(s_zw, done(l, s))
                    dve.wait_ge(s_a, freed(l, s, 2))
                    dve.tensor_reduce(logit[:, par, :], zw[:, :, :], axis=AX.X, op=ALU.add).then_inc(s_log, 1)
                    dve.wait_ge(s_a, done(l, s))
                    dve.wait_ge(s_hot, done(l, s))
                    dve.wait_ge(s_sc, freed(l, s, 2))
                    dve.tensor_tensor(ahot[:, par, :, :], hot[:, :, :],
                                      a[:, par, :].unsqueeze(2).to_broadcast([P, TILES, WIN]), ALU.mult).then_inc(s_ahot, 1)

                def add(s, k):
                    base = dve.value_load(base_i[0:1, bass.ds(s, 1)], min_val=0, max_val=N - 1)
                    dve.wait_ge(s_sc, done(l, s))
                    dve.wait_ge(s_acc, freed(l, s, 1))
                    win = acc[:, bass.ds(base, WIN)]
                    dve.tensor_tensor(win, win, out_ps[:, k % 2, 0:WIN], ALU.add).then_inc(s_acc, 1)

                for k in range(SLOTS):
                    step(0, k, k)
                    if k > 0:
                        add(k - 1, k - 1)
                with dve.Fori(1, ROUNDS) as i:
                    for k in range(SLOTS):
                        step(i, i * SLOTS + k, k)
                        add(i * SLOTS + (k - 1), (k - 1) % SLOTS)
                step(ROUNDS, ROUNDS * SLOTS, 0)
                add(ROUNDS * SLOTS - 1, SLOTS - 1)
                add(S - 1, 0)

                def window(s, v, c):
                    base = dve.value_load(base_i[0:1, bass.ds(s, 1)], min_val=0, max_val=N - 1)
                    at = c * BEYOND_STEPS
                    dve.wait_ge(s_bs, at + 1)
                    dve.wait_ge(s_bd, (c + 1) * 48)
                    dve.memset(woff[:, :], float(WIN))
                    dve.drain()
                    with dve.If(v > 0):
                        with dve.Fori(0, v) as _:
                            dve.tensor_scalar(woff[:, :], woff[:, :], float(WIN), None, ALU.add)
                            dve.drain()
                        dve.nop()
                    dve.tensor_scalar(pick[:, 0, :], rel[0][:, :], woff[0:WIN, :], pidx[0:WIN, :],
                                      ALU.subtract, ALU.is_equal)
                    dve.tensor_scalar(drel[:, :], rel_all[:, bass.ds(s * TILES, TILES)], woff[:, :], None, ALU.subtract)
                    dve.drain()
                    dve.tensor_tensor(hot[:, :, :], iota_w[:, :].unsqueeze(1).to_broadcast([P, TILES, WIN]),
                                      drel[:, :].unsqueeze(2).to_broadcast([P, TILES, WIN]), ALU.is_equal).then_inc(s_bs, 1)
                    dve.wait_ge(s_bs, at + 4)
                    dve.wait_ge(s_bg, (c + 1) * (16 * TILES))
                    dve.tensor_tensor(z[:, :, :], z_part(0), msg[0][:, :, 0:C], ALU.add)
                    dve.drain()
                    dve.scalar_tensor_tensor(zw[:, :, :], z[:, :, :], 0.0,
                                             wa2_b[:, :].unsqueeze(1).to_broadcast([P, TILES, C]), ALU.max, ALU.mult)
                    dve.drain()
                    dve.tensor_reduce(logit[:, 0, :], zw[:, :, :], axis=AX.X, op=ALU.add).then_inc(s_bs, 1)
                    dve.wait_ge(s_bs, at + 6)
                    dve.tensor_tensor(ahot[:, 0, :, :], hot[:, :, :],
                                      a[:, 0, :].unsqueeze(2).to_broadcast([P, TILES, WIN]), ALU.mult).then_inc(s_bs, 1)
                    dve.wait_ge(s_bs, at + 8)
                    row = nc.s_assert_within(base + v * WIN + WIN, 0, N - 1)
                    win = acc[:, bass.ds(row, WIN)]
                    dve.tensor_tensor(win, win, out_ps[:, 0, 0:WIN], ALU.add).then_inc(s_bs, 1)
                beyond(dve, l, window)
                dve.drain().then_inc(s_bi, 1)

                gain = lambda t: t[:, :].unsqueeze(1).to_broadcast([P, GB, C])
                with dve.Fori(0, GROUPS // 2) as q2:
                    for u in range(2):
                        q = q2 * 2 + u
                        n = (l * GROUPS + q) * (VSTEPS + 2)
                        grp = h[:, bass.ds(q * GB, GB), :]
                        dve.wait_ge(s_up, l * GROUPS + q + 1)
                        dve.wait_ge(s_us, n)
                        dve.tensor_tensor(o1[:, :, :], upd_ps[:, u, 0:CHUNK].rearrange("p (b c) -> p b c", c=C),
                                          gain(bias_b), ALU.add).then_inc(s_us, 1)
                        dve.wait_ge(s_us, n + 1)
                        centred(q, s_us, n + 1)
                        dve.tensor_reduce(st[:, 1, :], o1[:, :, :], axis=AX.X, op=ALU.add).then_inc(s_var, 1)
                        dve.wait_ge(s_root, l * GROUPS + q + 1)
                        dve.reciprocal(st[:, 3, :], st[:, 2, :]).then_inc(s_us, 1)
                        dve.wait_ge(s_us, n + 5)
                        dve.tensor_tensor(o1[:, :, :], o2[:, :, :], st[:, 3, :].unsqueeze(2).to_broadcast([P, GB, C]),
                                          ALU.mult).then_inc(s_us, 1)
                        dve.wait_ge(s_us, n + 6)
                        dve.tensor_tensor(o2[:, :, :], o1[:, :, :], gain(g_b), ALU.mult).then_inc(s_us, 1)
                        dve.wait_ge(s_us, n + 7)
                        dve.tensor_tensor(o1[:, :, :], o2[:, :, :], gain(b_b), ALU.add).then_inc(s_us, 1)
                        dve.wait_ge(s_us, n + 8)
                        dve.scalar_tensor_tensor(grp, o1[:, :, :], floor[:, bass.ds(l, 1)], grp,
                                                 ALU.max, ALU.add).then_inc(s_us, 1)
                dve.wait_ge(s_us, (l + 1) * (GROUPS * (VSTEPS + 2)))
                dve.sem_inc(s_h, 1)
            dve.wait_ge(s_xf, 32)
            dve.tensor_tensor(h[:, 0:FULL, :], h[:, 0:FULL, :], x_again()[:, 0:FULL, :], ALU.add).then_inc(s_fin, 1)
            dve.tensor_tensor(h[0:REST, FULL, :], h[0:REST, FULL, :], x_again()[0:REST, FULL, :], ALU.add).then_inc(s_fin, 1)


_WEIGHTS = ["W_node", "W_e1", "b_e1", "W_e2", "b_e2", "Wa1", "ba1", "Wa2", "ba2", "bias", "ln_g", "ln_b"]


def laid_out(inputs):
    keep = np.ascontiguousarray
    src, dst = np.asarray(inputs["src"]), np.asarray(inputs["dst"])
    w = {k: keep(inputs["L0_gnn_" + k]) for k in _WEIGHTS}
    return {
        "x_dram": keep(inputs["x"]),
        "src_t_dram": keep(src.reshape(-1, P).T),
        "dst_t_dram": keep(dst.reshape(-1, P).T),
        "dst_dram": keep(dst),
        "eattr_t_dram": keep(np.asarray(inputs["edge_attr_3"]).T),
        "w_node_dram": w["W_node"],
        "w_node_t_dram": keep(w["W_node"].transpose(0, 2, 1)),
        "w_e1_dram": w["W_e1"], "b_e1_dram": w["b_e1"], "w_e2_dram": w["W_e2"], "b_e2_dram": w["b_e2"],
        "wa1_dram": w["Wa1"], "ba1_dram": w["ba1"], "wa2_dram": w["Wa2"], "ba2_dram": w["ba2"],
        "bias_dram": w["bias"], "ln_g_dram": w["ln_g"], "ln_b_dram": w["ln_b"],
        "ident_dram": np.eye(P, dtype=np.float32),
        "ones_dram": np.ones((1, GB * P), np.float32),
    }


def kernel(**inputs):
    import concourse.bacc as _bacc
    from concourse.bass_utils import run_bass_kernel_spmd as _run

    arrays = laid_out(inputs)
    nc = _bacc.Bacc("TRN2", target_bir_lowering=False, num_devices=1)
    args = [nc.dram_tensor(k, a.shape, mybir.dt.from_np(a.dtype), kind="ExternalInput").ap() for k, a in arrays.items()]
    out = nc.dram_tensor("out_dram", arrays["x_dram"].shape, F32, kind="ExternalOutput").ap()
    gnn_kernel(nc, *args, out)
    return _run(nc, [arrays], core_ids=[0]).results[0]["out_dram"]
```

```python
from contextlib import ExitStack

import numpy as np

import concourse.bass as bass
from concourse import mybir

F32 = mybir.dt.float32
BF16 = mybir.dt.bfloat16
I32 = mybir.dt.int32
I16 = mybir.dt.int16
ALU = mybir.AluOpType
ACT = mybir.ActivationFunctionType
AX = mybir.AxisListType

P = 128
TILES = 5
EDGES = P * TILES
WIN = 32
WIN_BITS = 5
PARTS = 3
PICK = PARTS * WIN
TERMS = 6
SLOTS = 4
AHEAD = SLOTS - 1
GB = 7
EPS = 1e-5
START = SLOTS
BEYOND_STEPS = 9


def gnn_kernel(nc, x, src_t, dst_t, dst, eattr_t, w_node, w_node_t, w_e1, b_e1, w_e2, b_e2,
               wa1, ba1, wa2, ba2, bias, ln_g, ln_b, ident, ones, window_row, part_mask, ones_bf, out):
    N, C = x.shape
    L = w_node.shape[0]
    E = dst.shape[0]
    S = E // EDGES
    ROUNDS = S // SLOTS
    T = E // P
    BLOCKS = -(-N // P)
    GROUPS = BLOCKS // GB
    NPAD = BLOCKS * P
    FULL = N // P
    REST = N - FULL * P
    assert S * EDGES == E and S == ROUNDS * SLOTS + 1 and S % 5 == 0 and GROUPS * GB == BLOCKS
    assert GROUPS % 2 == 0 and REST > 0 and WIN == 1 << WIN_BITS
    SP_ROWS = S // 5
    COPIES = S + AHEAD
    CHUNK = GB * C
    A = eattr_t.shape[0]
    ATTR = TERMS * A
    K = PICK + ATTR + PARTS
    BOTTOM = slice(PICK, P)
    SPLIT = 625 if (A * E // P) % 625 == 0 else A * E // P // 15
    SPLITS = A * E // P // SPLIT
    assert SPLITS * SPLIT * P == A * E and K <= P and PICK % 32 == 0

    ctx = ExitStack()
    with ctx:
        sb = lambda name, shape, dt=F32: ctx.enter_context(nc.sbuf_tensor(name, shape, dt))
        ps = lambda name, shape: ctx.enter_context(nc.psum_tensor(name, shape, F32))
        sem = lambda name: ctx.enter_context(nc.semaphore(name))
        dram = lambda name, shape, dt=F32: nc.dram_tensor(name, shape, dt, kind="Internal").ap()

        table = dram("gather_table", [NPAD, 2 * C])
        ptable = dram("p_table", [NPAD, PARTS, C], BF16)
        attr_d = dram("attr_parts", [PARTS, A * E], BF16)
        rel_d = dram("dst_minus_base", [S, EDGES], I16)
        base_d = dram("base", [S])
        span_d = dram("span", [S])

        acc = sb("acc", [P, max(NPAD, 6400 + T)])
        h = sb("h", [P, BLOCKS, C])
        src_all = sb("src_all", [P, T + AHEAD * TILES], I32)
        rel_all = sb("rel_all", [P, T])
        base_i = sb("base_i", [1, S], I32)
        more_i = sb("more_i", [1, S], I32)
        first_i = sb("first_i", [1, S], I32)
        more_f = sb("more_f", [1, S])
        first_f = sb("first_f", [1, S])
        total_i = sb("total_i", [1, 1], I32)
        idn = sb("idn", [P, P])
        iota_w = sb("iota_w", [P, WIN])
        pidx = sb("pidx", [P, 1])
        eps_c = sb("eps_c", [P, 1])
        wn = sb("wn", [C + 1, 3 * C])
        wnt = sb("wnt", [C, C])
        wab = sb("wab", [C, 2 * C])
        mask = sb("mask", [P, PARTS])
        wraw = sb("wraw", [P, L, 2 * C])
        wlow = sb("wlow", [P, L, 2 * C])
        wpart = sb("wpart", [P, PARTS, L, 2 * C], BF16)
        wsel = sb("wsel", [P, 2, L, 2 * C])
        wrow = sb("wrow", [P, L, 2 * C], BF16)
        wo = sb("wo", [P, C])
        wa2_b = sb("wa2_b", [P, C])
        ba2_b = sb("ba2_b", [P, 1])
        bias_b = sb("bias_b", [P, C])
        g_b = sb("g_b", [P, C])
        b_b = sb("b_b", [P, C])
        floor = sb("floor", [P, L])
        idx = sb("idx", [P, SLOTS, TILES], I32)
        msg = [sb(f"msg{k}", [P, TILES, 3 * C]) for k in range(SLOTS)]
        rel = [sb(f"rel{k}", [PICK, EDGES], I16) for k in range(SLOTS)]
        left = [sb(f"left{k}", [P, EDGES], BF16) for k in range(SLOTS)]
        right = sb("right", [P, SLOTS, 2 * C], BF16)
        ain = sb("ain", [P, 2, SPLIT])
        alow = sb("alow", [P, SPLIT])
        apart = sb("apart", [P, 2, PARTS, SPLIT], BF16)
        z = sb("z", [P, TILES, C])
        zw = sb("zw", [P, TILES, C])
        logit = sb("logit", [P, 2, TILES])
        a = sb("a", [P, 2, TILES])
        hot = sb("hot", [P, 2, TILES, WIN])
        ahot = sb("ahot", [P, 2, TILES, WIN])
        woff = sb("woff", [P, 1])
        drel = sb("drel", [P, TILES])
        hs = sb("hs", [P, 2, GB, C])
        hT = sb("hT", [C + 1, 2, GB * P])
        tabs = sb("tabs", [P, 2, GB, 3 * C])
        plow = sb("plow", [P, GB, C])
        pparts = sb("pparts", [P, 2, GB, PARTS, C], BF16)
        accs = sb("accs", [P, 2, GB * P])
        o1 = sb("o1", [P, GB, C])
        o2 = sb("o2", [P, GB, C])
        st = sb("st", [P, 4, GB])

        zr_ps = ps("zr_ps", [P, 4, 512])
        out_ps = ps("out_ps", [P, 2, 512])
        upd_ps = ps("upd_ps", [P, 2, 512])

        s_in = sem("inputs_landed")
        s_x = sem("x_landed")
        s_const = sem("constants_made")
        s_fl = sem("flat_dst_step")
        s_base_w = sem("base_written")
        s_base_r = sem("base_read")
        s_prep = sem("dst_tables_ready")
        s_ln0 = sem("first_ln_step")
        s_ln0v = sem("first_variance_ready")
        s_ln0r = sem("first_root_ready")
        s_h = sem("h_ready")
        s_w = sem("weights_landed")
        s_comp = sem("composite_product_ready")
        s_wn = sem("composite_weights_ready")
        s_zero = sem("acc_zeroed")
        s_hs = sem("h_staged")
        s_tr = sem("h_transposed")
        s_ht = sem("hT_ready")
        s_tab = sem("table_product_ready")
        s_tabs = sem("table_staged")
        s_pp = sem("p_split_step")
        s_ai = [sem(f"attributes_landed{u}") for u in range(2)]
        s_as_ = sem("attribute_split_step")
        s_ao = [sem(f"attribute_parts_written{u}") for u in range(2)]
        s_we = sem("edge_weights_step")
        s_wer = sem("edge_weights_laid_out")
        s_tw = [sem(f"table_written{u}") for u in range(2)]
        s_idx = sem("indices_laid_out")
        s_mark = sem("waits_passed")
        s_gat = [sem(f"gathered{k}") for k in range(SLOTS)]
        s_ld = [sem(f"edge_loads_landed{k}") for k in range(SLOTS)]
        s_pick = sem("pick_ready")
        s_zr = sem("zr_ready")
        s_zsum = sem("z_summed")
        s_zw = sem("z_weighted")
        s_log = sem("logit_ready")
        s_r = sem("r_ready")
        s_a = sem("a_ready")
        s_hot = sem("hot_ready")
        s_ahot = sem("ahot_ready")
        s_sc = sem("messages_summed")
        s_acc = sem("acc_added")
        s_bd = sem("beyond_loads_landed")
        s_bg = sem("beyond_gathered")
        s_bs = sem("beyond_step")
        s_bi = sem("beyond_vector_step")
        s_as = sem("acc_staged")
        s_up = sem("update_product_ready")
        s_us = sem("update_step")
        s_var = sem("variance_ready")
        s_root = sem("root_ready")
        s_xf = sem("x_reloaded")
        s_fin = sem("output_ready")
        s_out = sem("output_written")

        block = ctx.enter_context(nc.Block())
        W_DMAS = 16 * 12
        LOADS = 16 * (2 + PARTS)
        IN_DMAS = 6 + SLOTS + 2 + 2 * TERMS + PARTS
        VSTEPS = 7
        LSTEPS = 5

        def done(l, s):
            return l * S + s + (START + 1)

        def freed(l, s, ring):
            return l * S + s + (START + 1 - ring)

        def uses(l, i, k):
            return l * (ROUNDS + (k == 0)) + i

        def mark(eng):
            eng.sem_inc(s_mark, 1)

        def supertiles(eng, *stages):
            last = S - 1 + max(lag for lag, _ in stages)
            for n in [*range(SLOTS)]:
                for lag, body in stages:
                    if n >= lag:
                        body(0, n - lag, n - lag)
            with eng.Fori(1, ROUNDS) as i:
                for k in range(SLOTS):
                    for lag, body in stages:
                        body(i + (k - lag) // SLOTS, i * SLOTS + (k - lag), (k - lag) % SLOTS)
            for n in range(ROUNDS * SLOTS, last + 1):
                for lag, body in stages:
                    if n - lag < S:
                        body((n - lag) // SLOTS, n - lag, (n - lag) % SLOTS)

        def beyond(eng, l, body):
            mark(eng)
            total = eng.value_load(total_i[0:1, 0:1], min_val=0, max_val=S * BLOCKS * (P // WIN))
            with eng.If(total > 0):
                with eng.Fori(0, S) as s:
                    more = eng.value_load(more_i[0:1, bass.ds(s, 1)], min_val=0, max_val=BLOCKS * (P // WIN))
                    with eng.If(more > 0):
                        first = eng.value_load(first_i[0:1, bass.ds(s, 1)], min_val=0,
                                               max_val=S * BLOCKS * (P // WIN))
                        with eng.Fori(0, more) as v:
                            body(s, v, l * total + first + v)
                        eng.nop()
                    eng.nop()
                eng.nop()
            eng.nop()

        def tab_view():
            return zr_ps[:, :, :].rearrange("p b (u f) -> p (b u) f", u=2)

        def zr_tile(par, j): return zr_ps[:, 2 * par + j // 4, (j % 4) * 2 * C:(j % 4 + 1) * 2 * C]
        def zr_all(par): return zr_ps[:, 2 * par:2 * par + 2, :].rearrange("p b (j f) -> p (b j) f", j=4)
        def z_part(par): return zr_all(par)[:, 0:TILES, 0:C]
        def r_part(par): return zr_all(par)[:, 0:TILES, C:2 * C]

        def dst_flat(): return acc[0:SP_ROWS, 0:5 * EDGES].bitcast(I32)
        def st_rel(): return acc[0:SP_ROWS, 3200:3200 + 5 * EDGES // 2].bitcast(I16)
        def st_base(): return acc[0:SP_ROWS, 4800:4805]
        def st_top(): return acc[0:SP_ROWS, 4808:4813]
        def st_span(): return acc[0:SP_ROWS, 4816:4821]
        def base_all(): return acc[:, 5000:5000 + S]
        def dst_cols(): return acc[:, 6400:6400 + T].bitcast(I32)
        def x_again(): return acc[:, 0:BLOCKS * C].rearrange("p (b c) -> p b c", c=C)

        @block.sync
        def _(sp):
            sp.dma_start(src_all[:, 0:T], src_t).then_inc(s_in, 16)
            sp.dma_start(acc[:, 6400:6400 + T].bitcast(I32), dst_t).then_inc(s_in, 16)
            sp.dma_start(acc[0:SP_ROWS, 0:5 * EDGES].bitcast(I32), dst.rearrange("(p n) -> p n", p=SP_ROWS)).then_inc(s_in, 16)
            sp.dma_start(idn[:, :], ident).then_inc(s_in, 16)
            sp.dma_start(hT[C:C + 1, 0, :], ones[0:1, 0:GB * P]).then_inc(s_in, 16)
            sp.dma_start(hT[C:C + 1, 1, :], ones[0:1, 0:GB * P]).then_inc(s_in, 16)
            for k in range(SLOTS):
                sp.dma_start(left[k][PICK + ATTR:K, :], ones_bf[0:PARTS, :]).then_inc(s_in, 16)
            sp.dma_start(pidx[:, :], window_row).then_inc(s_in, 16)
            sp.dma_start(mask[:, :], part_mask).then_inc(s_in, 16)
            sp.wait_ge(s_const, 1)
            for t in range(TERMS):
                rows = slice(PICK + t * A, PICK + (t + 1) * A)
                sp.dma_start(wraw[rows, :, 0:C], wa1[:, 2 * C:2 * C + A, :].rearrange("l a c -> a l c")).then_inc(s_in, 16)
                sp.dma_start(wraw[rows, :, C:2 * C], w_e1.rearrange("l a c -> a l c")).then_inc(s_in, 16)
            for t in range(PARTS):
                row_ = PICK + ATTR + t
                sp.dma_start(wraw[row_:row_ + 1, :, C:2 * C], b_e1.rearrange("(o l) c -> o l c", o=1)).then_inc(s_in, 16)
            sp.dma_start(h[:, 0:FULL, :], x[0:FULL * P, :].rearrange("(b p) c -> p b c", p=P)).then_inc(s_x, 16)
            sp.dma_start(h[0:REST, FULL, :], x[FULL * P:N, :]).then_inc(s_x, 16)
            sp.wait_ge(s_fl, 4)
            sp.dma_start(base_d.rearrange("(p n) -> p n", p=SP_ROWS), st_base()).then_inc(s_base_w, 16)
            sp.dma_start(span_d.rearrange("(p n) -> p n", p=SP_ROWS), st_span()).then_inc(s_base_w, 16)
            sp.dma_start(rel_d.rearrange("(p a) n -> p (a n)", p=SP_ROWS), st_rel()).then_inc(s_base_w, 16)
            sp.wait_ge(s_base_w, 48)
            sp.dma_start(base_all(), base_d.partition_broadcast(P)).then_inc(s_base_r, 16)
            sp.dma_start(more_f[0:1, :], span_d.rearrange("(a n) -> a n", a=1)).then_inc(s_base_r, 16)
            flat_in = eattr_t.rearrange("a e -> (a e)").rearrange("(p n) -> p n", p=P)
            flat_out = attr_d.rearrange("t (p n) -> p t n", p=P)

            def split_io(c, u, last):
                cols = lambda t, c_: t[..., bass.ds(c_ * SPLIT, SPLIT)]
                if not last:
                    sp.wait_ge(s_as_, 4 * c + 1)
                    mark(sp)
                    sp.dma_start(ain[:, 1 - u, :], flat_in[:, bass.ds(c * SPLIT + SPLIT, SPLIT)]).then_inc(s_ai[1 - u], 16)
                sp.wait_ge(s_as_, 4 * c + 5)
                mark(sp)
                sp.dma_start(flat_out[:, :, bass.ds(c * SPLIT, SPLIT)], apart[:, u, :, :]).then_inc(s_ao[u], 16)
            sp.dma_start(ain[:, 0, :], flat_in[:, 0:SPLIT]).then_inc(s_ai[0], 16)
            with sp.Fori(0, SPLITS // 2) as c2:
                for u in range(2):
                    split_io(c2 * 2 + u, u, False)
            split_io(SPLITS - 1, 0, True)
            for u in range(2):
                sp.wait_ge(s_ao[u], 16 * ((SPLITS + 1 - u) // 2) + 16)
            with sp.Fori(0, L) as l:
                sp.wait_ge(s_h, l + 1)
                row = lambda t: t[bass.ds(l, 1)]
                flat = lambda t: t[bass.ds(l, 1)].rearrange("a b c -> (a b) c")
                for dst_ap, src_ap in [
                        (wn[0:C, C:2 * C], flat(w_node)), (wnt[:, :], flat(w_node_t)),
                        (wn[C:C + 1, 0:C], row(ba1)), (wn[C:C + 1, C:2 * C], row(b_e2)),
                        (wab[:, C:2 * C], flat(wa1[:, 0:C])), (wab[:, 0:C], flat(wa1[:, C:2 * C])),
                        (wo[C:2 * C, :], flat(w_e2)),
                        (wa2_b[:, :], row(wa2.rearrange("l c a -> l (c a)")).to_broadcast([P, C])),
                        (ba2_b[:, :], row(ba2).to_broadcast([P, 1])),
                        (bias_b[:, :], row(bias).to_broadcast([P, C])),
                        (g_b[:, :], row(ln_g).to_broadcast([P, C])),
                        (b_b[:, :], row(ln_b).to_broadcast([P, C]))]:
                    sp.dma_start(dst_ap, src_ap).then_inc(s_w, 16)
                with sp.Fori(0, GROUPS // 2) as q2:
                    for u in range(2):
                        q = q2 * 2 + u
                        sp.wait_ge(s_tabs, l * GROUPS + q + 2)
                        rows = lambda t: t[bass.ds(q * (GB * P), GB * P)].rearrange("(b p) f -> p b f", p=P)
                        sp.dma_start(rows(table), tabs[:, u, :, 0:2 * C]).then_inc(s_tw[u], 16)
                        sp.wait_ge(s_pp, (l * GROUPS + q) * 4 + 5)
                        sp.dma_start(rows(ptable.rearrange("n t c -> n (t c)")),
                                     pparts[:, u, :, :, :].rearrange("p b t c -> p b (t c)")).then_inc(s_tw[u], 16)
                for u in range(2):
                    sp.wait_ge(s_tw[u], (l + 1) * (GROUPS * 16) + 32)
                mark(sp)

                attr_rows = attr_d.rearrange("t (a e) -> (t a) e", a=A)

                def loads(s, k, p_row, landed):
                    sp.dma_start(rel[k][:, :], rel_d[bass.ds(s, 1), :].to_broadcast([PICK, EDGES])).then_inc(landed, 16)
                    sp.dma_start(right[0:PICK, k, 0:C], ptable[bass.ds(p_row, WIN)].rearrange("n t c -> (n t) c")).then_inc(landed, 16)
                    at = PICK
                    for parts in range(PARTS, 0, -1):
                        sp.dma_start(left[k][at:at + parts * A, :],
                                     attr_rows[0:parts * A, bass.ds(s * EDGES, EDGES)]).then_inc(landed, 16)
                        at += parts * A

                def step(i, s, k):
                    base = sp.value_load(base_i[0:1, bass.ds(s, 1)], min_val=0, max_val=N - 1)
                    sp.wait_ge(s_zr, freed(l, s, SLOTS))
                    loads(s, k, base, s_ld[k])
                supertiles(sp, (0, step))

                def window(s, v, c):
                    base = sp.value_load(base_i[0:1, bass.ds(s, 1)], min_val=0, max_val=N - 1)
                    sp.wait_ge(s_bs, c * BEYOND_STEPS + 1)
                    row_ = nc.s_assert_within(base + v * WIN + WIN, 0, N - 1)
                    loads(s, 0, row_, s_bd)
                sp.wait_ge(s_acc, done(l, S - 1))
                beyond(sp, l, window)
            sp.wait_ge(s_h, L + 1)
            sp.dma_start(x_again()[:, 0:FULL, :], x[0:FULL * P, :].rearrange("(b p) c -> p b c", p=P)).then_inc(s_xf, 16)
            sp.dma_start(x_again()[0:REST, FULL, :], x[FULL * P:N, :]).then_inc(s_xf, 16)
            sp.wait_ge(s_fin, 2)
            sp.dma_start(out[0:FULL * P, :].rearrange("(b p) c -> p b c", p=P), h[:, 0:FULL, :]).then_inc(s_out, 16)
            sp.dma_start(out[FULL * P:N, :], h[0:REST, FULL, :]).then_inc(s_out, 16)
            sp.wait_ge(s_out, 32)

        @block.gpsimd
        def _(pool):
            pool.memset(wraw[:, :, :], 0.0)
            pool.memset(h[:, FULL, :], 0.0).then_inc(s_const, 1)
            pool.memset(src_all[:, T:], 0)
            pool.memset(wn[:, :], 0.0)
            pool.memset(right[:, :, :], 0.0)
            pool.memset(eps_c[:, :], EPS)
            for l in range(L):
                pool.memset(floor[:, l:l + 1], 0.0 if l < L - 1 else -3.0e38)
            pool.iota(iota_w[:, :], pattern=[[1, WIN]], base=0, channel_multiplier=0,
                      allow_small_or_imprecise_dtypes=True).then_inc(s_const, 1)
            for u in range(2):
                pool.sem_inc(s_ao[u], 16)
                pool.sem_inc(s_tw[u], 32)
            pool.sem_inc(s_as_, 1)
            pool.sem_inc(s_pp, 1)

            def split(out_parts, whole, low, chain, n):
                pool.tensor_copy(out_parts(0), whole).then_inc(chain, 1)
                pool.wait_ge(chain, n + 1)
                pool.tensor_tensor(low, whole, out_parts(0), ALU.subtract).then_inc(chain, 1)
                pool.wait_ge(chain, n + 2)
                mark(pool)
                pool.tensor_copy(out_parts(1), low).then_inc(chain, 1)
                pool.wait_ge(chain, n + 3)
                pool.tensor_tensor(out_parts(2), low, out_parts(1), ALU.subtract).then_inc(chain, 1)

            def split_chunk(c, i, u):
                pool.wait_ge(s_ai[u], 16 * i + 16)
                pool.wait_ge(s_ao[u], 16 * i + 16)
                pool.wait_ge(s_as_, 4 * c + 1)
                mark(pool)
                split(lambda t: apart[:, u, t, :], ain[:, u, :], alow[:, :], s_as_, 4 * c + 1)
            with pool.Fori(0, SPLITS // 2) as c2:
                for u in range(2):
                    split_chunk(c2 * 2 + u, c2, u)
            split_chunk(SPLITS - 1, SPLITS // 2, 0)
            with pool.Fori(0, L) as l:
                pool.wait_ge(s_h, l + 1)
                mark(pool)
                pool.memset(acc[:, :], 0.0).then_inc(s_zero, 1)
                with pool.Fori(0, GROUPS // 2) as q2:
                    for u in range(2):
                        q = q2 * 2 + u
                        pool.wait_ge(s_tabs, l * GROUPS + q + 2)
                        pool.wait_ge(s_tw[u], (l * (GROUPS // 2) + q2) * 32 + 32)
                        pool.wait_ge(s_pp, (l * GROUPS + q) * 4 + 1)
                        mark(pool)
                        split(lambda t: pparts[:, u, :, t, :], tabs[:, u, :, 2 * C:3 * C], plow[:, :, :],
                              s_pp, (l * GROUPS + q) * 4 + 1)
                for u in range(2):
                    pool.wait_ge(s_tw[u], (l + 1) * (GROUPS * 16) + 32)
                mark(pool)

                def gather(k, landed):
                    for j in range(TILES):
                        pool.indirect_dma_start(
                            out=msg[k][:, j, 0:2 * C], out_offset=None, in_=table,
                            in_offset=bass.IndirectOffsetOnAxis(ap=idx[:, k, j:j + 1], axis=0)).then_inc(landed, 16)

                def step(i, s, k):
                    pool.wait_ge(s_idx, l * COPIES + s + 1)
                    pool.wait_ge(s_sc, freed(l, s, SLOTS))
                    mark(pool)
                    gather(k, s_gat[k])
                supertiles(pool, (0, step))

                def window(s, v, c):
                    pool.wait_ge(s_bs, c * BEYOND_STEPS + 2)
                    mark(pool)
                    gather(0, s_bg)
                beyond(pool, l, window)

        @block.scalar
        def _(act):
            with act.Fori(0, GROUPS) as q:
                act.wait_ge(s_ln0v, q + 1)
                act.activation(st[:, 2, :], st[:, 1, :], ACT.Sqrt, bias=eps_c[:, :], scale=1.0 / C).then_inc(s_ln0r, 1)
            act.sem_inc(s_r, START)
            act.sem_inc(s_a, START)
            with act.Fori(0, L) as l:
                act.wait_ge(s_h, l + 1)
                with act.Fori(0, GROUPS // 2) as q2:
                    for u in range(2):
                        q = q2 * 2 + u
                        act.copy(hs[:, u, :, :], h[:, bass.ds(q * GB, GB), :]).then_inc(s_hs, 1)
                        act.wait_ge(s_tr, l * GROUPS + q + 1)
                        act.copy(hT[0:C, u, 0:512], out_ps[0:C, 0, :])
                        act.copy(hT[0:C, u, 512:GB * P], out_ps[0:C, 1, 0:GB * P - 512]).then_inc(s_ht, 1)

                def lay_out(i, s, k):
                    act.wait_ge(s_zsum, freed(l, s, SLOTS))
                    act.copy(idx[:, k, :], src_all[:, bass.ds(s * TILES, TILES)]).then_inc(s_idx, 1)
                for k in range(AHEAD):
                    lay_out(0, k, k)

                def relu_r(par, k):
                    act.activation(msg[k][:, :, 2 * C:3 * C], r_part(par), ACT.Relu).then_inc(s_r, 1)

                def take_r(i, s, k):
                    act.wait_ge(s_zr, done(l, s))
                    act.wait_ge(s_sc, freed(l, s, SLOTS))
                    relu_r(k % 2, k)

                def attention(i, s, k):
                    act.wait_ge(s_log, done(l, s))
                    act.wait_ge(s_ahot, freed(l, s, 2))
                    act.activation(a[:, k % 2, :], logit[:, k % 2, :], ACT.Sigmoid, bias=ba2_b[:, :]).then_inc(s_a, 1)

                def indices(i, s, k):
                    n = k + AHEAD
                    lay_out(i + n // SLOTS, s + AHEAD, n % SLOTS)
                supertiles(act, (0, take_r), (1, attention), (0, indices))

                def window(s, v, c):
                    act.wait_ge(s_bs, c * BEYOND_STEPS + 1)
                    act.copy(idx[:, 0, :], src_all[:, bass.ds(s * TILES, TILES)]).then_inc(s_bs, 1)
                    act.wait_ge(s_bs, c * BEYOND_STEPS + 4)
                    act.activation(msg[0][:, :, 2 * C:3 * C], r_part(0), ACT.Relu).then_inc(s_bs, 1)
                    act.wait_ge(s_bs, c * BEYOND_STEPS + 6)
                    act.activation(a[:, 0, :], logit[:, 0, :], ACT.Sigmoid, bias=ba2_b[:, :]).then_inc(s_bs, 1)
                act.wait_ge(s_acc, done(l, S - 1))
                beyond(act, l, window)
                act.wait_ge(s_bi, l + 1)
                with act.Fori(0, GROUPS // 2) as q2:
                    for u in range(2):
                        q = q2 * 2 + u
                        act.copy(accs[:, u, :], acc[:, bass.ds(q * (GB * P), GB * P)]).then_inc(s_as, 1)
                        act.wait_ge(s_var, l * GROUPS + q + 1)
                        act.activation(st[:, 2, :], st[:, 1, :], ACT.Sqrt, bias=eps_c[:, :], scale=1.0 / C).then_inc(s_root, 1)

        @block.tensor
        def _(pe):
            pe.sem_inc(s_zr, START)
            pe.sem_inc(s_sc, START)
            pe.wait_ge(s_in, IN_DMAS * 16)
            with pe.Fori(0, L) as l:
                pe.wait_ge(s_w, (l + 1) * W_DMAS)
                mark(pe)
                pe.matmul(upd_ps[0:C, 0, 0:2 * C], wnt[:, :], wab[:, :], start=True, stop=True).then_inc(s_comp, 1)
                pe.wait_ge(s_wn, l + 1)
                mark(pe)
                with pe.Fori(0, GROUPS // 2) as q2:
                    for u in range(2):
                        q = q2 * 2 + u
                        pe.wait_ge(s_hs, l * GROUPS + q + 1)
                        mark(pe)
                        for j in range(GB):
                            t = pe.transpose(out_ps[0:C, j // 4, (j % 4) * P:(j % 4 + 1) * P], hs[:, u, j, :], idn[:, :])
                        t.then_inc(s_tr, 1)
                        pe.wait_ge(s_ht, l * GROUPS + q + 1)
                        pe.wait_ge(s_tabs, l * GROUPS + q + 1)
                        for j in range(GB):
                            t = pe.matmul(tab_view()[:, j, 0:3 * C], hT[:, u, j * P:(j + 1) * P], wn[:, :],
                                          start=True, stop=True)
                        t.then_inc(s_tab, 1)
                pe.wait_ge(s_tabs, (l + 1) * GROUPS + 1)

                pe.wait_ge(s_wer, l + 1)

                def zr_product(par, k):
                    for j in range(TILES):
                        t = pe.matmul(zr_tile(par, j), left[k][0:K, j * P:(j + 1) * P], right[0:K, k, :],
                                      start=True, stop=True)
                    return t

                def message_sum(par, k):
                    for j in range(TILES):
                        t = pe.matmul(out_ps[:, par, 0:WIN], msg[k][:, j, C:3 * C], ahot[:, par, j, :],
                                      start=(j == 0), stop=(j == TILES - 1))
                    return t

                def products(i, s, k):
                    pe.wait_ge(s_ld[k], (uses(l, i, k) + 1) * LOADS)
                    pe.wait_ge(s_pick, done(l, s))
                    pe.wait_ge(s_zsum, freed(l, s, 2))
                    pe.wait_ge(s_r, freed(l, s, 2))
                    zr_product(k % 2, k).then_inc(s_zr, 1)

                def sums(i, s, k):
                    pe.wait_ge(s_ahot, done(l, s))
                    pe.wait_ge(s_r, done(l, s))
                    pe.wait_ge(s_acc, freed(l, s, 2))
                    message_sum(k % 2, k).then_inc(s_sc, 1)
                supertiles(pe, (0, products), (2, sums))

                def window(s, v, c):
                    pe.wait_ge(s_bs, c * BEYOND_STEPS + 3)
                    zr_product(0, 0).then_inc(s_bs, 1)
                    pe.wait_ge(s_bs, c * BEYOND_STEPS + 8)
                    message_sum(0, 0).then_inc(s_bs, 1)
                pe.wait_ge(s_acc, done(l, S - 1))
                beyond(pe, l, window)
                with pe.Fori(0, GROUPS // 2) as q2:
                    for u in range(2):
                        q = q2 * 2 + u
                        pe.wait_ge(s_as, l * GROUPS + q + 1)
                        for j in range(GB):
                            t = pe.matmul(upd_ps[:, u, j * C:(j + 1) * C], accs[:, u, j * P:(j + 1) * P], wo[:, :],
                                          start=True, stop=True)
                        t.then_inc(s_up, 1)

        @block.vector
        def _(dve):
            f3 = dst_flat().rearrange("p (a n) -> p a n", n=EDGES)
            dve.wait_ge(s_in, IN_DMAS * 16)
            dve.tensor_reduce(st_base(), f3, axis=AX.X, op=ALU.min).then_inc(s_fl, 1)
            dve.tensor_reduce(st_top(), f3, axis=AX.X, op=ALU.max).then_inc(s_fl, 1)
            dve.wait_ge(s_fl, 2)
            dve.tensor_tensor(st_span(), st_top(), st_base(), ALU.subtract).then_inc(s_fl, 1)
            dve.tensor_tensor(st_rel().rearrange("p (a n) -> p a n", n=EDGES), f3,
                              st_base().unsqueeze(2).to_broadcast([SP_ROWS, 5, EDGES]), ALU.subtract).then_inc(s_fl, 1)
            low = lambda t: t[BOTTOM]
            dve.tensor_copy(low(wpart)[:, 0], low(wraw)).then_inc(s_we, 1)
            dve.wait_ge(s_we, 1)
            dve.tensor_tensor(low(wlow), low(wraw), low(wpart)[:, 0], ALU.subtract).then_inc(s_we, 1)
            dve.wait_ge(s_we, 2)
            dve.tensor_copy(low(wpart)[:, 1], low(wlow)).then_inc(s_we, 1)
            dve.wait_ge(s_we, 3)
            dve.tensor_tensor(low(wpart)[:, 2], low(wlow), low(wpart)[:, 1], ALU.subtract).then_inc(s_we, 1)
            dve.tensor_scalar(low(wsel)[:, 0], low(wpart)[:, 0], mask[BOTTOM, 0:1], None, ALU.mult).then_inc(s_we, 1)
            dve.wait_ge(s_we, 5)
            dve.scalar_tensor_tensor(low(wsel)[:, 1], low(wpart)[:, 1], mask[BOTTOM, 1:2], low(wsel)[:, 0],
                                     ALU.mult, ALU.add).then_inc(s_we, 1)
            dve.wait_ge(s_we, 6)
            dve.scalar_tensor_tensor(low(wrow), low(wpart)[:, 2], mask[BOTTOM, 2:3], low(wsel)[:, 1],
                                     ALU.mult, ALU.add).then_inc(s_we, 1)
            dve.wait_ge(s_we, 7)
            dve.tensor_copy(wo[0:C, :], idn[0:C, 0:C]).then_inc(s_prep, 1)
            dve.wait_ge(s_base_r, 32)
            dve.tensor_tensor(rel_all[:, :].rearrange("p (s j) -> p s j", j=TILES),
                              dst_cols().rearrange("p (s j) -> p s j", j=TILES),
                              base_all().unsqueeze(2).to_broadcast([P, S, TILES]), ALU.subtract).then_inc(s_prep, 1)
            dve.tensor_copy(base_i[0:1, :], base_all()[0:1, :]).then_inc(s_prep, 1)
            dve.tensor_copy(more_i[0:1, :], more_f[0:1, :]).then_inc(s_prep, 1)
            dve.wait_ge(s_prep, 4)
            dve.tensor_scalar(first_i[0:1, :], more_i[0:1, :], WIN_BITS, None, ALU.arith_shift_right).then_inc(s_prep, 1)
            dve.wait_ge(s_prep, 5)
            dve.tensor_copy(more_i[0:1, :], first_i[0:1, :]).then_inc(s_prep, 1)
            dve.tensor_copy(more_f[0:1, :], first_i[0:1, :]).then_inc(s_prep, 1)
            dve.wait_ge(s_prep, 7)
            dve.tensor_tensor_scan(first_f[0:1, :], more_f[0:1, :], more_f[0:1, :], 0.0, ALU.add, ALU.bypass).then_inc(s_prep, 1)
            dve.wait_ge(s_prep, 8)
            dve.tensor_copy(total_i[0:1, :], first_f[0:1, S - 1:S]).then_inc(s_prep, 1)
            dve.tensor_tensor(first_i[0:1, :], first_f[0:1, :], more_f[0:1, :], ALU.subtract).then_inc(s_prep, 1)

            dve.wait_ge(s_x, 32)
            dve.wait_ge(s_const, 2)

            def centred(n, chain, total):
                dve.tensor_reduce(st[:, 0, :], o1[:, :, :], axis=AX.X, op=ALU.add).then_inc(chain, 1)
                dve.wait_ge(chain, total + 1)
                dve.scalar_tensor_tensor(o2[:, :, :], st[:, 0, :].unsqueeze(2).to_broadcast([P, GB, C]), -1.0 / C,
                                         o1[:, :, :], ALU.mult, ALU.add).then_inc(chain, 1)
                dve.wait_ge(chain, total + 2)
                dve.tensor_tensor(o1[:, :, :], o2[:, :, :], o2[:, :, :], ALU.mult).then_inc(chain, 1)
                dve.wait_ge(chain, total + 3)

            for s_ in (s_ln0, s_us, s_tabs, s_bs):
                dve.sem_inc(s_, 1)
            with dve.Fori(0, GROUPS) as q:
                n = q * (LSTEPS + 1) + 1
                grp = h[:, bass.ds(q * GB, GB), :]
                dve.wait_ge(s_ln0, n)
                dve.tensor_copy(o1[:, :, :], grp).then_inc(s_ln0, 1)
                dve.wait_ge(s_ln0, n + 1)
                centred(q, s_ln0, n + 1)
                dve.tensor_reduce(st[:, 1, :], o1[:, :, :], axis=AX.X, op=ALU.add).then_inc(s_ln0v, 1)
                dve.wait_ge(s_ln0r, q + 1)
                dve.reciprocal(st[:, 3, :], st[:, 2, :]).then_inc(s_ln0, 1)
                dve.wait_ge(s_ln0, n + 5)
                dve.scalar_tensor_tensor(grp, o2[:, :, :], 0.0, st[:, 3, :].unsqueeze(2).to_broadcast([P, GB, C]),
                                         ALU.max, ALU.mult).then_inc(s_ln0, 1)
            dve.wait_ge(s_ln0, GROUPS * (LSTEPS + 1) + 1)
            dve.wait_ge(s_prep, 10)
            dve.sem_inc(s_h, 1)
            for s_ in (s_pick, s_zsum, s_zw, s_log, s_hot, s_ahot, s_acc):
                dve.sem_inc(s_, START)

            with dve.Fori(0, L) as l:
                dve.wait_ge(s_comp, l + 1)
                dve.tensor_copy(wn[0:C, 0:C], upd_ps[0:C, 0, 0:C])
                dve.tensor_copy(wn[0:C, 2 * C:3 * C], upd_ps[0:C, 0, C:2 * C]).then_inc(s_wn, 1)
                with dve.Fori(0, GROUPS // 2) as q2:
                    for u in range(2):
                        q = q2 * 2 + u
                        dve.wait_ge(s_tab, l * GROUPS + q + 1)
                        dve.wait_ge(s_tw[u], (l * (GROUPS // 2) + q2) * 32 + 32)
                        dve.tensor_copy(tabs[:, u, :, :], tab_view()[:, 0:GB, 0:3 * C]).then_inc(s_tabs, 1)
                dve.tensor_copy(right[BOTTOM, :, :], wrow[BOTTOM, bass.ds(l, 1), :].to_broadcast([P - PICK, SLOTS, 2 * C])).then_inc(s_wer, 1)
                dve.wait_ge(s_zero, l + 1)

                def window_pick(i, s, k):
                    dve.wait_ge(s_ld[k], (uses(l, i, k) + 1) * LOADS)
                    dve.wait_ge(s_zr, freed(l, s, SLOTS))
                    dve.tensor_scalar(left[k][0:PICK, :], rel[k][:, :], pidx[0:PICK, :], None, ALU.is_equal).then_inc(s_pick, 1)

                def z_sum(i, s, k):
                    dve.wait_ge(s_r, done(l, s))
                    dve.wait_ge(s_gat[k], (uses(l, i, k) + 1) * (16 * TILES))
                    dve.wait_ge(s_zw, freed(l, s, 1))
                    dve.tensor_tensor(z[:, :, :], z_part(k % 2), msg[k][:, :, 0:C], ALU.add).then_inc(s_zsum, 1)

                def edge_hot(i, s, k):
                    dve.wait_ge(s_ahot, freed(l, s, 2))
                    dve.tensor_tensor(hot[:, k % 2, :, :], iota_w[:, :].unsqueeze(1).to_broadcast([P, TILES, WIN]),
                                      rel_all[:, bass.ds(s * TILES, TILES)].unsqueeze(2).to_broadcast([P, TILES, WIN]),
                                      ALU.is_equal).then_inc(s_hot, 1)

                def z_weighted(i, s, k):
                    dve.wait_ge(s_zsum, done(l, s))
                    dve.wait_ge(s_log, freed(l, s, 1))
                    dve.scalar_tensor_tensor(zw[:, :, :], z[:, :, :], 0.0,
                                             wa2_b[:, :].unsqueeze(1).to_broadcast([P, TILES, C]),
                                             ALU.max, ALU.mult).then_inc(s_zw, 1)

                def logits(i, s, k):
                    dve.wait_ge(s_zw, done(l, s))
                    dve.wait_ge(s_a, freed(l, s, 2))
                    dve.tensor_reduce(logit[:, k % 2, :], zw[:, :, :], axis=AX.X, op=ALU.add).then_inc(s_log, 1)

                def hot_times_a(i, s, k):
                    dve.wait_ge(s_a, done(l, s))
                    dve.wait_ge(s_hot, done(l, s))
                    dve.wait_ge(s_sc, freed(l, s, 2))
                    dve.tensor_tensor(ahot[:, k % 2, :, :], hot[:, k % 2, :, :],
                                      a[:, k % 2, :].unsqueeze(2).to_broadcast([P, TILES, WIN]), ALU.mult).then_inc(s_ahot, 1)

                def add(i, s, k):
                    base = dve.value_load(base_i[0:1, bass.ds(s, 1)], min_val=0, max_val=N - 1)
                    dve.wait_ge(s_sc, done(l, s))
                    dve.wait_ge(s_acc, freed(l, s, 1))
                    win = acc[:, bass.ds(base, WIN)]
                    dve.tensor_tensor(win, win, out_ps[:, k % 2, 0:WIN], ALU.add).then_inc(s_acc, 1)
                supertiles(dve, (0, window_pick), (1, z_sum), (1, edge_hot), (1, z_weighted), (2, hot_times_a),
                           (1, logits), (3, add))

                def window(s, v, c):
                    base = dve.value_load(base_i[0:1, bass.ds(s, 1)], min_val=0, max_val=N - 1)
                    at = c * BEYOND_STEPS + 1
                    dve.wait_ge(s_bs, at + 1)
                    dve.wait_ge(s_bd, (c + 1) * LOADS)
                    dve.memset(woff[:, :], float(WIN))
                    dve.drain()
                    with dve.If(v > 0):
                        with dve.Fori(0, v) as _:
                            dve.tensor_scalar(woff[:, :], woff[:, :], float(WIN), None, ALU.add)
                            dve.drain()
                        dve.nop()
                    dve.tensor_scalar(left[0][0:PICK, :], rel[0][:, :], woff[0:PICK, :], pidx[0:PICK, :],
                                      ALU.subtract, ALU.is_equal)
                    dve.tensor_scalar(drel[:, :], rel_all[:, bass.ds(s * TILES, TILES)], woff[:, :], None, ALU.subtract)
                    dve.drain()
                    dve.tensor_tensor(hot[:, 0, :, :], iota_w[:, :].unsqueeze(1).to_broadcast([P, TILES, WIN]),
                                      drel[:, :].unsqueeze(2).to_broadcast([P, TILES, WIN]), ALU.is_equal).then_inc(s_bs, 1)
                    dve.wait_ge(s_bs, at + 4)
                    dve.wait_ge(s_bg, (c + 1) * (16 * TILES))
                    dve.tensor_tensor(z[:, :, :], z_part(0), msg[0][:, :, 0:C], ALU.add)
                    dve.drain()
                    dve.scalar_tensor_tensor(zw[:, :, :], z[:, :, :], 0.0,
                                             wa2_b[:, :].unsqueeze(1).to_broadcast([P, TILES, C]), ALU.max, ALU.mult)
                    dve.drain()
                    dve.tensor_reduce(logit[:, 0, :], zw[:, :, :], axis=AX.X, op=ALU.add).then_inc(s_bs, 1)
                    dve.wait_ge(s_bs, at + 6)
                    dve.tensor_tensor(ahot[:, 0, :, :], hot[:, 0, :, :],
                                      a[:, 0, :].unsqueeze(2).to_broadcast([P, TILES, WIN]), ALU.mult).then_inc(s_bs, 1)
                    dve.wait_ge(s_bs, at + 8)
                    row = nc.s_assert_within(base + v * WIN + WIN, 0, N - 1)
                    win = acc[:, bass.ds(row, WIN)]
                    dve.tensor_tensor(win, win, out_ps[:, 0, 0:WIN], ALU.add).then_inc(s_bs, 1)
                beyond(dve, l, window)
                dve.drain().then_inc(s_bi, 1)

                gain = lambda t: t[:, :].unsqueeze(1).to_broadcast([P, GB, C])
                with dve.Fori(0, GROUPS // 2) as q2:
                    for u in range(2):
                        q = q2 * 2 + u
                        n = (l * GROUPS + q) * (VSTEPS + 2) + 1
                        grp = h[:, bass.ds(q * GB, GB), :]
                        dve.wait_ge(s_up, l * GROUPS + q + 1)
                        dve.wait_ge(s_us, n)
                        dve.tensor_tensor(o1[:, :, :], upd_ps[:, u, 0:CHUNK].rearrange("p (b c) -> p b c", c=C),
                                          gain(bias_b), ALU.add).then_inc(s_us, 1)
                        dve.wait_ge(s_us, n + 1)
                        centred(q, s_us, n + 1)
                        dve.tensor_reduce(st[:, 1, :], o1[:, :, :], axis=AX.X, op=ALU.add).then_inc(s_var, 1)
                        dve.wait_ge(s_root, l * GROUPS + q + 1)
                        dve.reciprocal(st[:, 3, :], st[:, 2, :]).then_inc(s_us, 1)
                        dve.wait_ge(s_us, n + 5)
                        dve.tensor_tensor(o1[:, :, :], o2[:, :, :], st[:, 3, :].unsqueeze(2).to_broadcast([P, GB, C]),
                                          ALU.mult).then_inc(s_us, 1)
                        dve.wait_ge(s_us, n + 6)
                        dve.tensor_tensor(o2[:, :, :], o1[:, :, :], gain(g_b), ALU.mult).then_inc(s_us, 1)
                        dve.wait_ge(s_us, n + 7)
                        dve.tensor_tensor(o1[:, :, :], o2[:, :, :], gain(b_b), ALU.add).then_inc(s_us, 1)
                        dve.wait_ge(s_us, n + 8)
                        dve.scalar_tensor_tensor(grp, o1[:, :, :], floor[:, bass.ds(l, 1)], grp,
                                                 ALU.max, ALU.add).then_inc(s_us, 1)
                dve.wait_ge(s_us, (l + 1) * (GROUPS * (VSTEPS + 2)) + 1)
                dve.sem_inc(s_h, 1)
            dve.wait_ge(s_xf, 32)
            dve.tensor_tensor(h[:, 0:FULL, :], h[:, 0:FULL, :], x_again()[:, 0:FULL, :], ALU.add).then_inc(s_fin, 1)
            dve.tensor_tensor(h[0:REST, FULL, :], h[0:REST, FULL, :], x_again()[0:REST, FULL, :], ALU.add).then_inc(s_fin, 1)


_WEIGHTS = ["W_node", "W_e1", "b_e1", "W_e2", "b_e2", "Wa1", "ba1", "Wa2", "ba2", "bias", "ln_g", "ln_b"]


def part_mask(attrs):
    part = [j for j in range(PARTS) for _ in range((PARTS - j) * attrs)] + list(range(PARTS))
    m = np.zeros((P, PARTS), np.float32)
    m[np.arange(PICK, PICK + len(part)), part] = 1.0
    return m


def laid_out(inputs):
    keep = np.ascontiguousarray
    src, dst = np.asarray(inputs["src"]), np.asarray(inputs["dst"])
    w = {k: keep(inputs["L0_gnn_" + k]) for k in _WEIGHTS}
    return {
        "x_dram": keep(inputs["x"]),
        "src_t_dram": keep(src.reshape(-1, P).T),
        "dst_t_dram": keep(dst.reshape(-1, P).T),
        "dst_dram": keep(dst),
        "eattr_t_dram": keep(np.asarray(inputs["edge_attr_3"]).T),
        "w_node_dram": w["W_node"],
        "w_node_t_dram": keep(w["W_node"].transpose(0, 2, 1)),
        "w_e1_dram": w["W_e1"], "b_e1_dram": w["b_e1"], "w_e2_dram": w["W_e2"], "b_e2_dram": w["b_e2"],
        "wa1_dram": w["Wa1"], "ba1_dram": w["ba1"], "wa2_dram": w["Wa2"], "ba2_dram": w["ba2"],
        "bias_dram": w["bias"], "ln_g_dram": w["ln_g"], "ln_b_dram": w["ln_b"],
        "ident_dram": np.eye(P, dtype=np.float32),
        "ones_dram": np.ones((1, GB * P), np.float32),
        "window_row_dram": (np.arange(P) // PARTS).astype(np.float32).reshape(P, 1),
        "part_mask_dram": part_mask(3),
        "ones_bf_dram": np.ones((PARTS, EDGES), mybir.dt.np(BF16)),
    }


def kernel(**inputs):
    import concourse.bacc as _bacc
    from concourse.bass_utils import run_bass_kernel_spmd as _run

    arrays = laid_out(inputs)
    nc = _bacc.Bacc("TRN2", target_bir_lowering=False, num_devices=1)
    args = [nc.dram_tensor(k, a.shape, mybir.dt.from_np(a.dtype), kind="ExternalInput").ap() for k, a in arrays.items()]
    out = nc.dram_tensor("out_dram", arrays["x_dram"].shape, F32, kind="ExternalOutput").ap()
    gnn_kernel(nc, *args, out)
    return _run(nc, [arrays], core_ids=[0]).results[0]["out_dram"]
```

```python
from contextlib import ExitStack

import numpy as np

import concourse.bass as bass
from concourse import mybir

F32 = mybir.dt.float32
BF16 = mybir.dt.bfloat16
I32 = mybir.dt.int32
I16 = mybir.dt.int16
ALU = mybir.AluOpType
ACT = mybir.ActivationFunctionType
AX = mybir.AxisListType

P = 128
TILES = 5
EDGES = P * TILES
WIN = 32
WIN_BITS = 5
PARTS = 3
PICK = PARTS * WIN
TERMS = 6
SLOTS = 4
AHEAD = SLOTS - 1
GB = 7
LB = 2
STRIDE = 12
SLACK = 8
LATE = 16384
EPS = 1e-5
START = SLOTS
NUMBERS = 6
PREP = 12
BEYOND_STEPS = 9


def gnn_kernel(nc, x, src_t, dst_t, dst, eattr_t, w_node, w_node_t, w_e1, b_e1, w_e2, b_e2,
               wa1, ba1, wa2, ba2, bias, ln_g, ln_b, ident, ones, window_row, part_mask, ones_bf, first_node, out):
    N, C = x.shape
    L = w_node.shape[0]
    E = dst.shape[0]
    S = E // EDGES
    ROUNDS = S // SLOTS
    T = E // P
    BLOCKS = -(-N // P)
    GROUPS = BLOCKS // GB
    LGROUPS = BLOCKS // LB
    ROWS = LB * P
    LATEST = latest(S, N)
    LOOPED = len(looped(S, N))
    NPAD = BLOCKS * P
    FULL = N // P
    REST = N - FULL * P
    assert S * EDGES == E and S == ROUNDS * SLOTS + 1 and S % 5 == 0 and GROUPS * GB == BLOCKS
    assert GROUPS % 2 == 0 and BLOCKS % LB == 0 and ROUNDS * SLOTS % STRIDE == 0 and N + LATE < 1 << 15
    assert REST > 0 and WIN == 1 << WIN_BITS
    SP_ROWS = S // 5
    COPIES = S + AHEAD
    AFTER = list(range(LOOPED, LGROUPS))
    TURNS = [LGROUPS - len(AFTER) // 2, len(AFTER) // 2]
    A = eattr_t.shape[0]
    MSG = TILES * 3 * C
    ACC = max(NPAD, 8200 + T)
    HALF = ACC // 2
    ATTR = TERMS * A
    K = PICK + ATTR + PARTS
    BOTTOM = slice(PICK, P)
    SPLIT = 625 if (A * E // P) % 625 == 0 else A * E // P // 15
    SPLITS = A * E // P // SPLIT
    BLANK = BLOCKS // (SPLITS - 1)
    assert SPLITS * SPLIT * P == A * E and SPLITS % 2 == 1 and BLANK * (SPLITS - 1) == BLOCKS and 6 * SPLIT <= SLOTS * MSG and K <= P and PICK % 32 == 0


    ctx = ExitStack()
    with ctx:
        sb = lambda name, shape, dt=F32: ctx.enter_context(nc.sbuf_tensor(name, shape, dt))
        ps = lambda name, shape: ctx.enter_context(nc.psum_tensor(name, shape, F32))
        sem = lambda name: ctx.enter_context(nc.semaphore(name))
        dram = lambda name, shape, dt=F32: nc.dram_tensor(name, shape, dt, kind="Internal").ap()

        table = dram("gather_table", [2 * NPAD, 2 * C])
        ptable = dram("p_table", [L * NPAD, PARTS, C], BF16)
        attr_d = dram("attr_parts", [PARTS, A * E], BF16)
        rel_d = dram("dst_minus_base", [S, EDGES], I16)
        number_d = dram("supertile_numbers", [NUMBERS, S])

        acc = sb("acc", [P, ACC])
        h = sb("h", [P, BLOCKS, C])

        src_all = sb("src_all", [P, T + AHEAD * TILES], I32)
        rel_all = sb("rel_all", [P, T])
        base_i = sb("base_i", [1, S], I32)
        start_i = sb("start_i", [1, S], I32)
        start_off = sb("start_off", [P, S])
        more_i = sb("more_i", [1, S], I32)
        first_i = sb("first_i", [1, S], I32)
        total_i = sb("total_i", [1, 1], I32)
        idn = sb("idn", [P, P])
        iota_w = sb("iota_w", [P, WIN])
        pidx = sb("pidx", [P, 1])
        eps_c = sb("eps_c", [P, 1])
        wn = sb("wn", [C + 1, L, 3 * C])
        wnt = sb("wnt", [C, L, C])
        wab = sb("wab", [C, L, 2 * C])
        mask = sb("mask", [P, PARTS])
        wraw = sb("wraw", [P, L, 2 * C])
        wlow = sb("wlow", [P, L, 2 * C])
        wpart = sb("wpart", [P, PARTS, L, 2 * C], BF16)
        wsel = sb("wsel", [P, 2, L, 2 * C])
        wrow = sb("wrow", [P, L, 2 * C], BF16)
        wo = sb("wo", [P, L, C])
        every = sb("every", [P, L, 4 * C + 3])
        ba2_all = sb("ba2_all", [P, L])
        cur = sb("cur", [P, 4 * C + 3])
        idx = sb("idx", [P, SLOTS, TILES], I32)
        msg_all = sb("msg_all", [P, SLOTS * TILES * 3 * C])
        msg = [msg_all[:, k * MSG:(k + 1) * MSG].rearrange("p (j f) -> p j f", j=TILES)
               for k in range(SLOTS)]
        rel = [sb(f"rel{k}", [PICK, EDGES], I16) for k in range(SLOTS)]
        left = [sb(f"left{k}", [P, EDGES], BF16) for k in range(SLOTS)]
        right = sb("right", [P, SLOTS, 2 * C], BF16)
        ain = msg_all[:, 0:2 * SPLIT].rearrange("p (u n) -> p u n", u=2)
        alow = msg_all[:, 2 * SPLIT:3 * SPLIT]
        apart = msg_all[:, 3 * SPLIT:6 * SPLIT].bitcast(BF16).rearrange("p (u t n) -> p u t n", u=2, t=PARTS)
        z = sb("z", [P, TILES, C])
        zw = sb("zw", [P, TILES, C])
        logit = sb("logit", [P, 2, TILES])
        a = sb("a", [P, 2, TILES])
        hot = sb("hot", [P, 2, TILES, WIN])
        ahot = sb("ahot", [P, 2, TILES, WIN])
        woff = sb("woff", [P, 1])
        drel = sb("drel", [P, TILES])
        hs = sb("hs", [P, 2, GB, C])
        hT = sb("hT", [C + 1, 2, GB * P])
        tabs = sb("tabs", [P, 2, GB, 3 * C])
        plow = sb("plow", [P, GB, C])
        pparts = sb("pparts", [P, 2, GB, PARTS, C], BF16)
        accs = sb("accs", [P, 2, ROWS])
        o1 = sb("o1", [P, GB, C])
        o2 = sb("o2", [P, GB, C])
        st = sb("st", [P, 4, GB])
        p1 = sb("p1", [P, 2, LB, C])
        p2 = sb("p2", [P, 2, LB, C])
        pst = sb("pst", [P, 2, 4, LB])
        zeros = sb("zeros", [P, ROWS])
        xg = sb("xg", [P, 2, LB, C])

        zr_ps = ps("zr_ps", [P, 4, 512])
        out_ps = ps("out_ps", [P, 2, 512])
        upd_ps = ps("upd_ps", [P, 2, 512])

        s_in = sem("inputs_landed")
        s_dst = sem("flat_dst_landed")
        s_x = sem("x_landed")
        s_const = sem("constants_made")
        s_fl = sem("flat_dst_step")
        s_base_w = sem("base_written")
        s_base_r = sem("base_read")
        s_prep = sem("dst_tables_ready")
        s_ln0 = sem("first_ln_step")
        s_ln0v = sem("first_variance_ready")
        s_ln0r = sem("first_root_ready")
        s_w = sem("weights_landed")
        s_comp = sem("composite_product_ready")
        s_wn = sem("composite_weights_ready")
        s_zero = sem("acc_zeroed")
        s_hs = sem("h_staged")
        s_tr = sem("h_transposed")
        s_ht = sem("hT_ready")
        s_tab = sem("table_product_ready")
        s_tabs = sem("table_staged")
        s_pp = sem("p_split_step")
        s_ai = [sem(f"attributes_landed{u}") for u in range(2)]
        s_as_ = sem("attribute_split_step")
        s_ao = [sem(f"attribute_parts_written{u}") for u in range(2)]
        s_we = sem("edge_weights_step")
        s_wer = sem("edge_weights_laid_out")
        s_tw = [sem(f"table_written{u}") for u in range(2)]
        s_idx = sem("indices_laid_out")
        s_mark = sem("waits_passed")
        s_gat = [sem(f"gathered{k}") for k in range(SLOTS)]
        s_ld = [sem(f"edge_loads_landed{k}") for k in range(SLOTS)]
        s_pick = sem("pick_ready")
        s_zr = sem("zr_ready")
        s_zsum = sem("z_summed")
        s_zw = sem("z_weighted")
        s_log = sem("logit_ready")
        s_r = sem("r_ready")
        s_a = sem("a_ready")
        s_hot = sem("hot_ready")
        s_ahot = sem("ahot_ready")
        s_sc = sem("messages_summed")
        s_acc = sem("acc_added")
        s_bd = sem("beyond_loads_landed")
        s_bg = sem("beyond_gathered")
        s_br = sem("beyond_rows_landed")

        s_bs = sem("beyond_step")
        s_bi = sem("beyond_vector_step")
        s_as = sem("acc_staged")
        s_clear = sem("acc_group_cleared")
        s_up = sem("update_product_ready")
        s_ua = sem("update_step_a")
        s_var = sem("variance_ready")
        s_root = sem("root_ready")
        s_ub = sem("update_step_b")
        s_lhs = sem("new_h_staged")
        s_ltr = sem("new_h_transposed")
        s_lht = sem("new_hT_ready")
        s_ltp = sem("new_table_product_ready")
        s_lt = sem("new_tables_step")
        s_lw = [sem(f"new_tables_written{u}") for u in range(2)]
        s_xg = [sem(f"x_group_landed{u}") for u in range(2)]
        s_o = sem("output_group_ready")
        s_out = [sem(f"output_written{u}") for u in range(2)]
        s_blank = sem("odd_layers_table_blank")
        s_src = sem("src_landed")
        s_lp = [sem(f"new_p_table_written{u}") for u in range(2)]
        s_cur = sem(
"layer_constants_ready")

        block = ctx.enter_context(nc.Block())
        W_DMAS = 16 * (9 + 3 * L)
        LOADS = 16 * (2 + PARTS)
        IN_DMAS = 4 + SLOTS + 2 + 2 * TERMS + PARTS
        ASTEPS, BSTEPS, TSTEPS = 4, 5, 5
        LSTEPS = 5

        def done(l, s):
            return l * S + s + (START + 1)

        def freed(l, s, ring):
            return l * S + s + (START + 1 - ring)

        def uses(l, i, k):
            return l * (ROUNDS + (k == 0)) + i

        def mark(eng):
            eng.sem_inc(s_mark, 1)

        def supertiles(eng, stages, nodes=()):
            last = S - 1 + max((lag for lag, _ in stages), default=0)

            def rounds(i, first):
                for k in range(SLOTS):
                    for lag, body in stages:
                        body(i + (k - lag) // SLOTS, i * SLOTS + (k - lag), (k - lag) % SLOTS)
                    if first is not None:
                        g, r = first
                        for at, body in nodes:
                            if at == r * SLOTS + k:
                                body(g - LATEST, 0, g - LATEST, g * STRIDE - 1)
            for n in [*range(SLOTS)]:
                for lag, body in stages:
                    if n >= lag:
                        body(0, n - lag, n - lag)
            per = STRIDE // SLOTS
            plain = min(LATEST * per, ROUNDS) if nodes else ROUNDS
            with eng.Fori(1, plain) as i:
                rounds(i, None)
            if nodes and LOOPED:
                with eng.Fori(LATEST, LATEST + LOOPED) as g:
                    for r in range(per):
                        rounds(g * per + r, (g, r))
            for n in range(ROUNDS * SLOTS, last + 1):
                for lag, body in stages:
                    if n - lag < S:
                        body((n - lag) // SLOTS, n - lag, (n - lag) % SLOTS)
            turns = sorted((STRIDE * (e // 2 * 2) + at + e % 2, e, order) for e in range(len(AFTER))
                           for order, (at, _) in enumerate(nodes))
            for _, e, order in turns:
                nodes[order][1](AFTER[e], e % 2, e // 2 + (LOOPED if e % 2 == 0 else 0), S - 1)

        def first_groups(eng, *stages):
            last = GROUPS - 1 + max(lag for lag, _ in stages)
            peel = -(-max(lag for lag, _ in stages) // 2) * 2
            for n in range(peel):
                for lag, body in stages:
                    if n >= lag:
                        body(n - lag, (n - lag) // 2, (n - lag) % 2)
            with eng.Fori(peel // 2, GROUPS // 2) as q2:
                for u in range(2):
                    for lag, body in stages:
                        body(q2 * 2 + (u - lag), q2 + (u - lag) // 2, (u - lag) % 2)
            for n in range(GROUPS, last + 1):
                for lag, body in stages:
                    if n - lag < GROUPS:
                        body(n - lag, (n - lag) // 2, (n - lag) % 2)

        def first_transpose_bank(u):
            return (upd_ps, out_ps)[u]

        def group_done(l, q):
            return l * LGROUPS + q + 2

        def group_freed(l, q, u):
            return l * LGROUPS + q + (1 - u)

        def composite(l):
            return upd_ps[0:C, l // 2, (l % 2) * 2 * C:(l % 2 + 1) * 2 * C]

        def update_bank(u):
            return (upd_ps, out_ps)[u][:, 0, :]

        def transpose_bank(u):
            return (upd_ps, out_ps)[u][0:C, 1, 0:ROWS]

        def acc_group(q):
            return acc[:, bass.ds(q * ROWS, ROWS)]

        def h_group(q):
            return h[:, bass.ds(q * LB, LB), :]

        def beyond(eng, l, body):
            mark(eng)
            total = eng.value_load(total_i[0:1, 0:1], min_val=0, max_val=S * BLOCKS * (P // WIN))
            with eng.If(total > 0):
                with eng.Fori(0, S) as s:
                    more = eng.value_load(more_i[0:1, bass.ds(s, 1)], min_val=0, max_val=BLOCKS * (P // WIN))
                    with eng.If(more > 0):
                        first = eng.value_load(first_i[0:1, bass.ds(s, 1)], min_val=0,
                                               max_val=S * BLOCKS * (P // WIN))
                        with eng.Fori(0, more) as v:
                            body(s, v, l * total + first + v)
                        eng.nop()
                    eng.nop()
                eng.nop()
            eng.nop()

        def tab_view():
            return zr_ps[:, :, :].rearrange("p b (u f) -> p (b u) f", u=2)

        def zr_tile(par, j): return zr_ps[:, 2 * par + j // 4, (j % 4) * 2 * C:(j % 4 + 1) * 2 * C]
        def zr_all(par): return zr_ps[:, 2 * par:2 * par + 2, :].rearrange("p b (j f) -> p (b j) f", j=4)
        def z_part(par): return zr_all(par)[:, 0:TILES, 0:C]
        def r_part(par): return zr_all(par)[:, 0:TILES, C:2 * C]

        def dst_flat(): return acc[0:SP_ROWS, 0:5 * EDGES].bitcast(I32)
        def st_rel(): return acc[0:SP_ROWS, 3200:3200 + 5 * EDGES // 2].bitcast(I16)
        def number(r): return acc[0:SP_ROWS, 4800:4800 + NUMBERS * 5].rearrange("p (r n) -> p r n", n=5)[:, r, :]
        def numbers(): return acc[0:SP_ROWS, 4800:4800 + NUMBERS * 5].rearrange("p (r n) -> p r n", n=5)
        def st_base(): return acc[0:SP_ROWS, 4840:4845]
        def st_top(): return acc[0:SP_ROWS, 4845:4850]
        def st_first(): return acc[0:SP_ROWS, 4850:4855]
        def st_next(): return acc[0:SP_ROWS, 4855:4860]
        def off_all(): return acc[:, 5000:5000 + S]
        def number_row(r): return acc[0:1, 5640 + (r - 2) * S:5640 + (r - 1) * S]
        def dst_cols(): return acc[:, 8200:8200 + T].bitcast(I32)

        wa2_c, bias_c, g_c, b_c = (cur[:, n * C:(n + 1) * C] for n in range(4))
        ba2_c, floor_c, row_c = (cur[:, 4 * C + n:4 * C + n + 1] for n in range(3))

        @block.sync
        def _(sp):
            flat_in = eattr_t.rearrange("a e -> (a e)").rearrange("(p n) -> p n", p=P)
            flat_out = attr_d.rearrange("t (p n) -> p t n", p=P)
            sp.dma_start(dst_flat(), dst.rearrange("(p n) -> p n", p=SP_ROWS)).then_inc(s_dst, 16)
            sp.dma_start(st_first(), first_node.rearrange("(p n) -> p n", p=SP_ROWS)).then_inc(s_dst, 16)
            for u in range(2):
                sp.dma_start(ain[:, u, :], flat_in[:, u * SPLIT:(u + 1) * SPLIT]).then_inc(s_ai[u], 16)
            sp.wait_ge(s_const, 1)
            sp.dma_start(h[:, 0:FULL, :], x[0:FULL * P, :].rearrange("(b p) c -> p b c", p=P)).then_inc(s_x, 16)
            sp.dma_start(h[0:REST, FULL, :], x[FULL * P:N, :]).then_inc(s_x, 16)
            sp.dma_start(dst_cols(), dst_t).then_inc(s_in, 16)
            for k in range(SLOTS):
                sp.dma_start(left[k][PICK + ATTR:K, :], ones_bf[0:PARTS, :]).then_inc(s_in, 16)
            sp.dma_start(pidx[:, :], window_row).then_inc(s_in, 16)
            def split_io(c, u, more, piece):
                sp.wait_ge(s_as_, 4 * c + 5)
                mark(sp)
                sp.dma_start(flat_out[:, :, bass.ds(c * SPLIT, SPLIT)], apart[:, u, :, :]).then_inc(s_ao[u], 16)
                if more:
                    sp.dma_start(ain[:, u, :], flat_in[:, bass.ds(c * SPLIT + 2 * SPLIT, SPLIT)]).then_inc(s_ai[u], 16)
                if piece:
                    sp.dma_start(table[bass.ds(NPAD + c * BLANK * P, BLANK * P)].rearrange("(b p) f -> p b f", p=P),
                                 zeros[:, 0:2 * C].unsqueeze(1).to_broadcast([P, BLANK, 2 * C])).then_inc(s_blank, 16)
            split_io(0, 0, True, True)
            sp.dma_start(src_all[:, 0:T], src_t).then_inc(s_src, 16)
            sp.wait_ge(s_base_w, 32)
            sp.dma_start(off_all(), number_d[0].partition_broadcast(P)).then_inc(s_base_r, 16)
            sp.dma_start(start_off[:, :], number_d[1].partition_broadcast(P)).then_inc(s_base_r, 16)
            sp.dma_start(acc[0:1, 5640:5640 + (NUMBERS - 2) * S], number_d[2:NUMBERS].rearrange("r n -> (r n)").unsqueeze(0)).then_inc(s_base_r, 16)
            split_io(1, 1, True, True)
            with sp.Fori(1, SPLITS // 2 - 1) as c2:
                for u in range(2):
                    split_io(c2 * 2 + u, u, True, True)
            split_io(SPLITS - 3, 0, True, True)
            split_io(SPLITS - 2, 1, False, True)
            split_io(SPLITS - 1, 0, False, False)
            for u in range(2):
                sp.wait_ge(s_ao[u], 16 * ((SPLITS + 1 - u) // 2) + 16)
            for u in range(2):
                sp.wait_ge(s_tw[u], GROUPS * 16 + 32)
            sp.wait_ge(s_prep, PREP)
            with sp.Fori(0, L) as l:
                for u in range(2):
                    sp.wait_ge(s_lp[u], l * TURNS[u] * 16 + 16)
                sp.wait_ge(s_acc, done(l, -1))
                mark(sp)

                attr_rows = attr_d.rearrange("t (a e) -> (t a) e", a=A)

                def loads(s, k, p_row, landed):
                    sp.dma_start(rel[k][:, :], rel_d[bass.ds(s, 1), :].to_broadcast([PICK, EDGES])).then_inc(landed, 16)
                    sp.dma_start(right[0:PICK, k, 0:C], ptable[bass.ds(p_row, WIN)].rearrange("n t c -> (n t) c")).then_inc(landed, 16)
                    at = PICK
                    for parts in range(PARTS, 0, -1):
                        sp.dma_start(left[k][at:at + parts * A, :],
                                     attr_rows[0:parts * A, bass.ds(s * EDGES, EDGES)]).then_inc(landed, 16)
                        at += parts * A

                def window(s, v, c):
                    node = sp.value_load(start_i[0:1, bass.ds(s, 1)], min_val=0, max_val=N + WIN)
                    sp.wait_ge(s_bs, c * BEYOND_STEPS + 1)
                    row_ = nc.s_assert_within(node + v * WIN + l * NPAD, 0, L * NPAD - WIN)
                    loads(s, 0, row_, s_bd)
                beyond(sp, l, window)
                sp.wait_ge(s_bi, l + 1)
                mark(sp)


                def step(i, s, k):
                    base = sp.value_load(base_i[0:1, bass.ds(s, 1)], min_val=0, max_val=N - 1)
                    sp.wait_ge(s_zr, freed(l, s, SLOTS))
                    loads(s, k, nc.s_assert_within(base + l * NPAD, 0, L * NPAD - WIN), s_ld[k])
                supertiles(sp, [(0, step)])
            for u in range(2):
                sp.wait_ge(s_out[u], 16 + 16 * TURNS[u] + (16 if (len(AFTER) - 1) % 2 == u else 0))

        @block.gpsimd
        def _(pool):
            pool.memset(wraw[:, :, :], 0.0)
            pool.memset(wn[:, :, :], 0.0)
            pool.memset(h[:, FULL, :], 0.0).then_inc(s_const, 1)
            pool.memset(src_all[:, T:], 0)
            pool.memset(zeros[:, :], 0.0)
            pool.memset(xg[:, :, :, :], 0.0)
            pool.memset(right[:, :, :], 0.0)
            pool.memset(eps_c[:, :], EPS)
            for l in range(L):
                pool.memset(every[:, l, 4 * C + 1:4 * C + 2], 0.0 if l < L - 1 else -3.0e38)
                pool.memset(every[:, l, 4 * C + 2:4 * C + 3], float(l % 2 * NPAD))
            pool.iota(iota_w[:, :], pattern=[[1, WIN]], base=0, channel_multiplier=0,
                      allow_small_or_imprecise_dtypes=True).then_inc(s_const, 1)
            for u in range(2):
                pool.sem_inc(s_ao[u], 16)
                pool.sem_inc(s_tw[u], 32)
            pool.sem_inc(s_as_, 1)

            def split(out_parts, whole, low, chain, n):
                pool.tensor_copy(out_parts(0), whole).then_inc(chain, 1)
                pool.wait_ge(chain, n + 1)
                pool.tensor_tensor(low, whole, out_parts(0), ALU.subtract).then_inc(chain, 1)
                pool.wait_ge(chain, n + 2)
                mark(pool)
                pool.tensor_copy(out_parts(1), low).then_inc(chain, 1)
                pool.wait_ge(chain, n + 3)
                pool.tensor_tensor(out_parts(2), low, out_parts(1), ALU.subtract).then_inc(chain, 1)

            def split_chunk(c, i, u):
                pool.wait_ge(s_ai[u], 16 * i + 16)
                pool.wait_ge(s_ao[u], 16 * i + 16)
                pool.wait_ge(s_as_, 4 * c + 1)
                mark(pool)
                split(lambda t: apart[:, u, t, :], ain[:, u, :], alow[:, :], s_as_, 4 * c + 1)
            with pool.Fori(0, SPLITS // 2) as c2:
                for u in range(2):
                    split_chunk(c2 * 2 + u, c2, u)
            split_chunk(SPLITS - 1, SPLITS // 2, 0)
            pool.wait_ge(s_prep, PREP)
            mark(pool)
            pool.memset(acc[:, 0:HALF], 0.0).then_inc(s_zero, 1)
            pool.wait_ge(s_blank, 16 * (SPLITS - 1))
            for u in range(2):
                pool.wait_ge(s_ao[u], 16 * ((SPLITS + 1 - u) // 2) + 16)

            for u in range(2):
                pool.wait_ge(s_tw[u], GROUPS * 16 + 32)
            with pool.Fori(0, L) as l:
                for u in range(2):
                    pool.wait_ge(s_lw[u], l * TURNS[u] * 16 + 16)
                mark(pool)

                def gather(k, landed):
                    for j in range(TILES):
                        pool.indirect_dma_start(
                            out=msg[k][:, j, 0:2 * C], out_offset=None, in_=table,
                            in_offset=bass.IndirectOffsetOnAxis(ap=idx[:, k, j:j + 1], axis=0)).then_inc(landed, 16)

                def window(s, v, c):
                    pool.wait_ge(s_bs, c * BEYOND_STEPS + 2)
                    mark(pool)
                    gather(0, s_bg)
                    pool.wait_ge(s_bg, 16 * TILES)
                    mark(pool)
                    pool.inc_swdge_sem([s_bg], [16 * TILES], mode="sub")
                    pool.sem_inc(s_br, 1)
                beyond(pool, l, window)
                pool.wait_ge(s_bi, l + 1)

                def step(i, s, k):
                    pool.wait_ge(s_idx, l * COPIES + s + 1)
                    pool.wait_ge(s_sc, freed(l, s, SLOTS))
                    mark(pool)
                    gather(k, s_gat[k])
                supertiles(pool, [(0, step)])

        @block.scalar
        def _(act):
            act.dma_start(mask[:, :], part_mask).then_inc(s_in, 16)
            act.dma_start(idn[:, :], ident).then_inc(s_in, 16)
            act.dma_start(hT[C:C + 1, 0, :], ones[0:1, 0:GB * P]).then_inc(s_in, 16)
            act.dma_start(hT[C:C + 1, 1, :], ones[0:1, 0:GB * P]).then_inc(s_in, 16)
            act.wait_ge(s_const, 1)
            for t in range(TERMS):
                rows = slice(PICK + t * A, PICK + (t + 1) * A)
                act.dma_start(wraw[rows, :, 0:C], wa1[:, 2 * C:2 * C + A, :].rearrange("l a c -> a l c")).then_inc(s_in, 16)
                act.dma_start(wraw[rows, :, C:2 * C], w_e1.rearrange("l a c -> a l c")).then_inc(s_in, 16)
            for t in range(PARTS):
                row_ = PICK + ATTR + t
                act.dma_start(wraw[row_:row_ + 1, :, C:2 * C], b_e1.rearrange("(o l) c -> o l c", o=1)).then_inc(s_in, 16)
            for dst_ap, src_ap in [
                    (wnt[:, :, :], w_node_t.rearrange("l a b -> a l b")),
                    (wab[:, :, C:2 * C], wa1[:, 0:C].rearrange("l a b -> a l b")),
                    (wab[:, :, 0:C], wa1[:, C:2 * C].rearrange("l a b -> a l b")),
                    (wo[C:2 * C, :, :], w_e2.rearrange("l a b -> a l b")),
                    (every[:, :, 0:C], wa2.rearrange("l c a -> a l c").to_broadcast([P, L, C])),
                    (every[:, :, C:2 * C], bias.unsqueeze(0).to_broadcast([P, L, C])),
                    (every[:, :, 2 * C:3 * C], ln_g.unsqueeze(0).to_broadcast([P, L, C])),
                    (every[:, :, 3 * C:4 * C], ln_b.unsqueeze(0).to_broadcast([P, L, C])),
                    (ba2_all[:, :], ba2.rearrange("l a -> a l").to_broadcast([P, L]))]:
                act.dma_start(dst_ap, src_ap).then_inc(s_w, 16)
            for l in range(L):
                at = (l - 1) % L
                act.dma_start(wn[0:C, at, C:2 * C], w_node[l]).then_inc(s_w, 16)
                act.dma_start(wn[C:C + 1, at, 0:C], ba1[l:l + 1]).then_inc(s_w, 16)
                act.dma_start(wn[C:C + 1, at, C:2 * C], b_e2[l:l + 1]).then_inc(s_w, 16)
            act.wait_ge(s_fl, 10)
            act.dma_start(number_d.rearrange("r (p n) -> p r n", p=SP_ROWS), numbers()).then_inc(s_base_w, 16)
            act.dma_start(rel_d.rearrange("(p a) n -> p (a n)", p=SP_ROWS), st_rel()).then_inc(s_base_w, 16)
            act.sem_inc(s_tabs, 1)
            act.sem_inc(s_r, START)
            act.sem_inc(s_a, START)
            for s_ in (s_as, s_root, s_lhs, s_lht):
                act.sem_inc(s_, 1)

            def first_hT(q, i, u):
                act.wait_ge(s_tr, q + 1)
                act.copy(hT[0:C, u, 0:512], first_transpose_bank(u)[0:C, 0, :])
                act.copy(hT[0:C, u, 512:GB * P], first_transpose_bank(u)[0:C, 1, 0:GB * P - 512]).then_inc(s_ht, 1)

            def first_root(q, i, u):
                act.wait_ge(s_ln0v, q + 1)
                act.activation(st[:, 2, :], st[:, 1, :], ACT.Sqrt, bias=eps_c[:, :], scale=1.0 / C).then_inc(s_ln0r, 1)

            def first_stage(q, i, u):
                act.wait_ge(s_ln0, (q + 1) * LSTEPS + 1)
                act.copy(hs[:, u, :, :], h[:, bass.ds(q * GB, GB), :]).then_inc(s_hs, 1)

            def first_rows(q, i, u):
                act.wait_ge(s_tab, q + 1)
                act.wait_ge(s_tw[u], i * 32 + 32)
                act.copy(tabs[:, u, :, :], tab_view()[:, 0:GB, 0:3 * C]).then_inc(s_tabs, 1)

            def first_store(q, i, u):
                rows = lambda t: t[bass.ds(q * (GB * P), GB * P)].rearrange("(b p) f -> p b f", p=P)
                act.wait_ge(s_pp, q * 4 + 5)
                act.dma_start(rows(table), tabs[:, u, :, 0:2 * C]).then_inc(s_tw[u], 16)
                act.dma_start(rows(ptable.rearrange("n t c -> n (t c)")),
                              pparts[:, u, :, :, :].rearrange("p b t c -> p b (t c)")).then_inc(s_tw[u], 16)
            first_groups(act, (1, first_hT), (0, first_root), (0, first_stage), (3, first_store), (2, first_rows))
            act.wait_ge(s_prep, PREP)
            act.wait_ge(s_const, 2)
            act.copy(acc[:, HALF:], zeros[:, 0:1].to_broadcast([P, ACC - HALF])).then_inc(s_zero, 1)
            act.wait_ge(s_src, 16)
            with act.Fori(0, L) as l:
                act.wait_ge(s_acc, done(l, -1))
                act.wait_ge(s_cur, l + 1)

                def index_rows(k, s):
                    return act.activation(idx[:, k, :], src_all[:, bass.ds(s * TILES, TILES)], ACT.Identity,
                                          bias=row_c)

                def window(s, v, c):
                    act.wait_ge(s_bs, c * BEYOND_STEPS + 1)
                    index_rows(0, s).then_inc(s_bs, 1)
                    act.wait_ge(s_bs, c * BEYOND_STEPS + 4)
                    act.activation(msg[0][:, :, 2 * C:3 * C], r_part(0), ACT.Relu).then_inc(s_bs, 1)
                    act.wait_ge(s_bs, c * BEYOND_STEPS + 6)
                    act.activation(a[:, 0, :], logit[:, 0, :], ACT.Sigmoid, bias=ba2_c).then_inc(s_bs, 1)
                beyond(act, l, window)
                act.wait_ge(s_bi, l + 1)

                def lay_out(i, s, k):
                    act.wait_ge(s_zsum, freed(l, s, SLOTS))
                    index_rows(k, s).then_inc(s_idx, 1)
                for k in range(AHEAD):
                    lay_out(0, k, k)

                def take_r(i, s, k):
                    act.wait_ge(s_zr, done(l, s))
                    act.wait_ge(s_sc, freed(l, s, SLOTS))
                    act.activation(msg[k][:, :, 2 * C:3 * C], r_part(k % 2), ACT.Relu).then_inc(s_r, 1)

                def attention(i, s, k):
                    act.wait_ge(s_log, done(l, s))
                    act.wait_ge(s_ahot, freed(l, s, 2))
                    act.activation(a[:, k % 2, :], logit[:, k % 2, :], ACT.Sigmoid, bias=ba2_c).then_inc(s_a, 1)

                def indices(i, s, k):
                    n = k + AHEAD
                    lay_out(i + n // SLOTS, s + AHEAD, n % SLOTS)

                def stage_acc(q, u, v, s):
                    act.wait_ge(s_acc, done(l, s))
                    act.wait_ge(s_up, group_freed(l, q, u))
                    act.copy(accs[:, u, :], acc_group(q)).then_inc(s_as, 1)

                def load_x(q, u, v, s):
                    with act.If(l > L - 2):
                        act.wait_ge(s_o, q + (1 - u))
                        if isinstance(q, int) and q == LGROUPS - 1:
                            act.dma_start(xg[:, u, 0, :], x[FULL * P - P:FULL * P, :]).then_inc(s_xg[u], 16)
                            act.dma_start(xg[0:REST, u, 1, :], x[FULL * P:N, :]).then_inc(s_xg[u], 16)
                        else:
                            act.dma_start(xg[:, u, :, :], x[bass.ds(q * ROWS, ROWS)].rearrange("(b p) c -> p b c", p=P)).then_inc(s_xg[u], 16)
                    act.nop()

                def root(q, u, v, s):
                    act.wait_ge(s_var, l * LGROUPS + q + 1)
                    act.activation(pst[:, u, 2, :], pst[:, u, 1, :], ACT.Sqrt, bias=eps_c[:, :], scale=1.0 / C).then_inc(s_root, 1)

                def stage_h(q, u, v, s):
                    with act.If(l < L - 1):
                        act.wait_ge(s_ub, (l * LGROUPS + q + 1) * BSTEPS + 1)
                        act.wait_ge(s_ltr, group_freed(l, q, u))
                        act.copy(hs[:, u, 0:LB, :], h_group(q)).then_inc(s_lhs, 1)
                    act.nop()

                def take_hT(q, u, v, s):
                    with act.If(l < L - 1):
                        act.wait_ge(s_ltr, group_done(l, q))
                        act.wait_ge(s_ltp, group_freed(l, q, u))
                        act.copy(hT[0:C, u, 0:ROWS], transpose_bank(u)).then_inc(s_lht, 1)
                    act.nop()

                def store(q, u, v, s):
                    with act.If(l < L - 1):
                        rows = lambda t, row: t[bass.ds(row, ROWS)].rearrange("(b p) f -> p b f", p=P)
                        act.wait_ge(s_lt, (l * LGROUPS + q) * TSTEPS + 2)
                        act.dma_start(rows(table, ((l + 1) & 1) * NPAD + q * ROWS), tabs[:, u, 0:LB, 0:2 * C]).then_inc(s_lw[u], 16)
                        act.wait_ge(s_lt, (l * LGROUPS + q + 1) * TSTEPS + 1)
                        act.dma_start(rows(ptable.rearrange("n t c -> n (t c)"),
                                           nc.s_assert_within(l * NPAD + (q * ROWS + NPAD), 0, L * NPAD - ROWS)),
                                      pparts[:, u, 0:LB, :, :].rearrange("p b t c -> p b (t c)")).then_inc(s_lp[u], 16)
                    act.nop()
                    with act.If(l > L - 2):
                        act.wait_ge(s_o, q + 2)
                        if isinstance(q, int) and q == LGROUPS - 1:
                            act.dma_start(out[FULL * P - P:FULL * P, :], tabs[:, u, 0, 0:C]).then_inc(s_out[u], 16)
                            act.dma_start(out[FULL * P:N, :], tabs[0:REST, u, 1, 0:C]).then_inc(s_out[u], 16)
                        else:
                            act.dma_start(out[bass.ds(q * ROWS, ROWS)].rearrange("(b p) c -> p b c", p=P),
                                          tabs[:, u, 0:LB, 0:C]).then_inc(s_out[u], 16)
                    act.nop()
                supertiles(act, [(0, take_r), (1, attention), (0, indices)],
                           [(2, stage_acc), (3, load_x), (5, root), (7, stage_h), (9, take_hT), (11, store)])

        @block.tensor
        def _(pe):
            pe.sem_inc(s_zr, START)
            pe.sem_inc(s_sc, START)
            pe.wait_ge(s_in, IN_DMAS * 16)
            for s_ in (s_up, s_ltr, s_ltp):
                pe.sem_inc(s_, 1)
            pe.wait_ge(s_w, W_DMAS)
            for l in range(L):
                t = pe.matmul(composite(l),
                              wnt[:, l, :], wab[:, l, :], start=True, stop=True)
            t.then_inc(s_comp, 1)
            pe.wait_ge(s_wn, 1)
            mark(pe)

            def first_transposes(q, i, u):
                pe.wait_ge(s_hs, q + 1)
                mark(pe)
                for j in range(GB):
                    t = pe.transpose(first_transpose_bank(u)[0:C, j // 4, (j % 4) * P:(j % 4 + 1) * P], hs[:, u, j, :], idn[:, :])
                t.then_inc(s_tr, 1)

            def first_product(q, i, u):
                pe.wait_ge(s_ht, q + 1)
                pe.wait_ge(s_tabs, q + 1)
                for j in range(GB):
                    t = pe.matmul(tab_view()[:, j, 0:3 * C], hT[:, u, j * P:(j + 1) * P], wn[:, L - 1, :],
                                  start=True, stop=True)
                t.then_inc(s_tab, 1)
            first_groups(pe, (0, first_transposes), (1, first_product))
            pe.wait_ge(s_tabs, GROUPS + 1)
            pe.wait_ge(s_prep, PREP)
            with pe.Fori(0, L) as l:
                pe.wait_ge(s_acc, done(l, -1))
                pe.wait_ge(s_wer, l + 1)

                def zr_product(par, k):
                    for j in range(TILES):
                        t = pe.matmul(zr_tile(par, j), left[k][0:K, j * P:(j + 1) * P], right[0:K, k, :],
                                      start=True, stop=True)
                    return t

                def message_sum(par, k):
                    for j in range(TILES):
                        t = pe.matmul(out_ps[:, par, 0:WIN], msg[k][:, j, C:3 * C], ahot[:, par, j, :],
                                      start=(j == 0), stop=(j == TILES - 1))
                    return t

                def window(s, v, c):
                    pe.wait_ge(s_bs, c * BEYOND_STEPS + 3)
                    zr_product(0, 0).then_inc(s_bs, 1)
                    pe.wait_ge(s_bs, c * BEYOND_STEPS + 8)
                    message_sum(0, 0).then_inc(s_bs, 1)
                beyond(pe, l, window)
                pe.wait_ge(s_bi, l + 1)

                def products(i, s, k):
                    pe.wait_ge(s_ld[k], (uses(l, i, k) + 1) * LOADS)
                    pe.wait_ge(s_pick, done(l, s))
                    pe.wait_ge(s_zsum, freed(l, s, 2))
                    pe.wait_ge(s_r, freed(l, s, 2))
                    zr_product(k % 2, k).then_inc(s_zr, 1)

                def sums(i, s, k):
                    pe.wait_ge(s_ahot, done(l, s))
                    pe.wait_ge(s_r, done(l, s))
                    pe.wait_ge(s_acc, freed(l, s, 2))
                    message_sum(k % 2, k).then_inc(s_sc, 1)
                def update_product(q, u, v, s):
                    pe.wait_ge(s_as, group_done(l, q))
                    for j in range(LB):
                        t = pe.matmul(update_bank(u)[:, j * C:(j + 1) * C], accs[:, u, j * P:(j + 1) * P],
                                      wo[:, bass.ds(l, 1), :], start=True, stop=True)
                    t.then_inc(s_up, 1)

                def table_product(q, u, v, s):
                    with pe.If(l < L - 1):
                        pe.wait_ge(s_lhs, group_done(l, q))
                        mark(pe)
                        for j in range(LB):
                            t = pe.transpose(transpose_bank(u)[:, j * P:(j + 1) * P], hs[:, u, j, :], idn[:, :])
                        t.then_inc(s_ltr, 1)
                        pe.wait_ge(s_lht, group_done(l, q))
                        for j in range(LB):
                            at = LB * C + j * 3 * C
                            t = pe.matmul(update_bank(u)[:, at:at + 3 * C], hT[:, u, j * P:(j + 1) * P],
                                          wn[:, bass.ds(l, 1), :], start=True, stop=True)
                        t.then_inc(s_ltp, 1)
                    pe.nop()
                supertiles(pe, [(0, products), (2, sums)], [(3, update_product), (9, table_product)])

        @block.vector
        def _(dve):
            f3 = dst_flat().rearrange("p (a n) -> p a n", n=EDGES)
            dve.wait_ge(s_dst, 32)
            dve.tensor_reduce(st_base(), f3, axis=AX.X, op=ALU.min).then_inc(s_fl, 1)
            dve.tensor_reduce(st_top(), f3, axis=AX.X, op=ALU.max).then_inc(s_fl, 1)
            dve.wait_ge(s_fl, 2)
            dve.tensor_tensor(number(4), st_top(), st_base(), ALU.subtract).then_inc(s_fl, 1)
            dve.tensor_tensor(number(5), st_base(), st_first(), ALU.is_lt).then_inc(s_fl, 1)
            dve.tensor_tensor(number(2), st_base(), st_first(), ALU.max).then_inc(s_fl, 1)
            dve.tensor_scalar(st_next(), st_base(), float(WIN), None, ALU.add).then_inc(s_fl, 1)
            dve.wait_ge(s_fl, 6)
            dve.scalar_tensor_tensor(number(0), number(5), -float(LATE), st_base(), ALU.mult, ALU.add).then_inc(s_fl, 1)
            dve.scalar_tensor_tensor(number(3), number(5), -float(WIN), st_next(), ALU.mult, ALU.add).then_inc(s_fl, 1)
            dve.tensor_scalar(number(1), number(5), float(LATE - WIN), float(WIN), ALU.mult, ALU.add).then_inc(s_fl, 1)
            dve.wait_ge(s_fl, 9)
            dve.tensor_tensor(st_rel().rearrange("p (a n) -> p a n", n=EDGES), f3,
                              number(0).unsqueeze(2).to_broadcast([SP_ROWS, 5, EDGES]), ALU.subtract).then_inc(s_fl, 1)
            dve.wait_ge(s_in, IN_DMAS * 16)
            low = lambda t: t[BOTTOM]
            dve.tensor_copy(low(wpart)[:, 0], low(wraw)).then_inc(s_we, 1)
            dve.wait_ge(s_we, 1)
            dve.tensor_tensor(low(wlow), low(wraw), low(wpart)[:, 0], ALU.subtract).then_inc(s_we, 1)
            dve.wait_ge(s_we, 2)
            dve.tensor_copy(low(wpart)[:, 1], low(wlow)).then_inc(s_we, 1)
            dve.wait_ge(s_we, 3)
            dve.tensor_tensor(low(wpart)[:, 2], low(wlow), low(wpart)[:, 1], ALU.subtract).then_inc(s_we, 1)
            dve.tensor_scalar(low(wsel)[:, 0], low(wpart)[:, 0], mask[BOTTOM, 0:1], None, ALU.mult).then_inc(s_we, 1)
            dve.wait_ge(s_we, 5)
            dve.scalar_tensor_tensor(low(wsel)[:, 1], low(wpart)[:, 1], mask[BOTTOM, 1:2], low(wsel)[:, 0],
                                     ALU.mult, ALU.add).then_inc(s_we, 1)
            dve.wait_ge(s_we, 6)
            dve.scalar_tensor_tensor(low(wrow), low(wpart)[:, 2], mask[BOTTOM, 2:3], low(wsel)[:, 1],
                                     ALU.mult, ALU.add).then_inc(s_we, 1)
            dve.wait_ge(s_we, 7)
            dve.tensor_copy(wo[0:C, :, :], idn[0:C, 0:C].unsqueeze(1).to_broadcast([C, L, C])).then_inc(s_prep, 1)
            dve.wait_ge(s_const, 2)

            def squares(raw, sq, mid, stats, width, chain, n):
                dve.tensor_reduce(stats[:, 0, :], raw, axis=AX.X, op=ALU.add).then_inc(chain, 1)
                dve.wait_ge(chain, n + 1)
                dve.scalar_tensor_tensor(mid, stats[:, 0, :].unsqueeze(2).to_broadcast([P, width, C]), -1.0 / C,
                                         raw, ALU.mult, ALU.add).then_inc(chain, 1)
                dve.wait_ge(chain, n + 2)
                dve.tensor_tensor(sq, mid, mid, ALU.mult).then_inc(chain, 1)
                dve.wait_ge(chain, n + 3)
                return dve.tensor_reduce(stats[:, 1, :], sq, axis=AX.X, op=ALU.add)

            for s_ in (s_ln0, s_pp, s_bs, s_ua, s_ub, s_lt, s_clear, s_o):
                dve.sem_inc(s_, 1)
            for s_ in (s_pick, s_zsum, s_zw, s_log, s_hot, s_ahot, s_acc):
                dve.sem_inc(s_, START)
            for u in range(2):
                dve.sem_inc(s_lw[u], 16)
                dve.sem_inc(s_lp[u], 16)
                dve.sem_inc(s_out[u], 16)
            dve.wait_ge(s_comp, 1)
            dve.tensor_copy(every[:, :, 4 * C:4 * C + 1], ba2_all[:, :].unsqueeze(2))
            for l in range(L):

                at = (l - 1) % L
                dve.tensor_copy(wn[0:C, at, 0:C], composite(l)[:, 0:C])
                dve.tensor_copy(wn[0:C, at, 2 * C:3 * C], composite(l)[:, C:2 * C])
            dve.drain().then_inc(s_wn, 1)

            def first_centre(q, i, u):
                n = q * LSTEPS + 1
                dve.wait_ge(s_ln0, n)
                squares(h[:, bass.ds(q * GB, GB), :], o1[:, :, :], o2[:, :, :], st, GB, s_ln0, n).then_inc(s_ln0v, 1)

            def first_h(q, i, u):
                n = q * LSTEPS + 1
                dve.wait_ge(s_ln0r, q + 1)
                dve.reciprocal(st[:, 3, :], st[:, 2, :]).then_inc(s_ln0, 1)
                dve.wait_ge(s_ln0, n + 4)
                dve.scalar_tensor_tensor(h[:, bass.ds(q * GB, GB), :], o2[:, :, :], 0.0,
                                         st[:, 3, :].unsqueeze(2).to_broadcast([P, GB, C]),
                                         ALU.max, ALU.mult).then_inc(s_ln0, 1)

            def p_parts(part, whole, low, chain, n):
                dve.wait_ge(chain, n)
                dve.tensor_copy(part(0), whole).then_inc(chain, 1)
                dve.wait_ge(chain, n + 1)
                dve.tensor_tensor(low, whole, part(0), ALU.subtract).then_inc(chain, 1)
                dve.wait_ge(chain, n + 2)
                dve.tensor_copy(part(1), low).then_inc(chain, 1)
                dve.wait_ge(chain, n + 3)
                dve.tensor_tensor(part(2), low, part(1), ALU.subtract).then_inc(chain, 1)

            def first_parts(q, i, u):
                dve.wait_ge(s_tabs, q + 2)
                p_parts(lambda t: pparts[:, u, :, t, :], tabs[:, u, :, 2 * C:3 * C], plow[:, :, :], s_pp, q * 4 + 1)
            dve.wait_ge(s_x, 32)
            first_groups(dve, (0, first_centre), (3, first_parts), (0, first_h))
            dve.wait_ge(s_base_r, 48)
            dve.tensor_tensor(rel_all[:, :].rearrange("p (s j) -> p s j", j=TILES),
                              dst_cols().rearrange("p (s j) -> p s j", j=TILES),
                              off_all().unsqueeze(2).to_broadcast([P, S, TILES]), ALU.subtract).then_inc(s_prep, 1)
            dve.tensor_copy(base_i[0:1, :], number_row(2)).then_inc(s_prep, 1)
            dve.tensor_copy(start_i[0:1, :], number_row(3)).then_inc(s_prep, 1)
            dve.tensor_copy(more_i[0:1, :], number_row(4)).then_inc(s_prep, 1)
            dve.wait_ge(s_prep, 5)
            dve.tensor_scalar(first_i[0:1, :], more_i[0:1, :], WIN_BITS, None, ALU.arith_shift_right).then_inc(s_prep, 1)
            dve.wait_ge(s_prep, 6)
            dve.tensor_copy(number_row(4), first_i[0:1, :]).then_inc(s_prep, 1)
            dve.wait_ge(s_prep, 7)
            dve.tensor_tensor(number_row(2), number_row(4), number_row(5), ALU.add).then_inc(s_prep, 1)
            dve.wait_ge(s_prep, 8)
            dve.tensor_copy(more_i[0:1, :], number_row(2)).then_inc(s_prep, 1)
            dve.tensor_tensor_scan(number_row(3), number_row(2), number_row(2), 0.0, ALU.add, ALU.bypass).then_inc(s_prep, 1)
            dve.wait_ge(s_prep, 10)
            dve.tensor_copy(total_i[0:1, :], number_row(3)[:, S - 1:S]).then_inc(s_prep, 1)
            dve.tensor_tensor(first_i[0:1, :], number_row(3), number_row(2), ALU.subtract).then_inc(s_prep, 1)
            dve.wait_ge(s_ln0, GROUPS * LSTEPS + 1)
            for u in range(2):
                dve.wait_ge(s_tw[u], GROUPS * 16 + 32)
            dve.wait_ge(s_zero, 2)
            dve.wait_ge(s_prep, PREP)
            with dve.Fori(0, L) as l:
                dve.wait_ge(s_ub, l * LGROUPS * BSTEPS + 1)
                dve.wait_ge(s_clear, l * LGROUPS + 1)
                dve.wait_ge(s_acc, done(l, -1))
                dve.tensor_copy(cur[:, :], every[:, bass.ds(l, 1), :]).then_inc(s_cur, 1)
                dve.tensor_copy(right[BOTTOM, :, :], wrow[BOTTOM, bass.ds(l, 1), :].to_broadcast([P - PICK, SLOTS, 2 * C])).then_inc(s_wer, 1)
                dve.wait_ge(s_cur, l + 1)

                def window(s, v, c):
                    node = dve.value_load(start_i[0:1, bass.ds(s, 1)], min_val=0, max_val=N + WIN)
                    at = c * BEYOND_STEPS + 1
                    dve.wait_ge(s_bs, at + 1)
                    dve.wait_ge(s_bd, (c + 1) * LOADS)
                    dve.tensor_copy(woff[:, :], start_off[:, bass.ds(s, 1)])
                    dve.drain()
                    with dve.If(v > 0):
                        with dve.Fori(0, v) as _:
                            dve.tensor_scalar(woff[:, :], woff[:, :], float(WIN), None, ALU.add)
                            dve.drain()
                        dve.nop()
                    dve.tensor_scalar(left[0][0:PICK, :], rel[0][:, :], woff[0:PICK, :], pidx[0:PICK, :],
                                      ALU.subtract, ALU.is_equal)
                    dve.tensor_scalar(drel[:, :], rel_all[:, bass.ds(s * TILES, TILES)], woff[:, :], None, ALU.subtract)
                    dve.drain()
                    dve.tensor_tensor(hot[:, 0, :, :], iota_w[:, :].unsqueeze(1).to_broadcast([P, TILES, WIN]),
                                      drel[:, :].unsqueeze(2).to_broadcast([P, TILES, WIN]), ALU.is_equal).then_inc(s_bs, 1)
                    dve.wait_ge(s_bs, at + 4)
                    dve.wait_ge(s_br, c + 1)
                    dve.tensor_tensor(z[:, :, :], z_part(0), msg[0][:, :, 0:C], ALU.add)
                    dve.drain()
                    dve.scalar_tensor_tensor(zw[:, :, :], z[:, :, :], 0.0,
                                             wa2_c.unsqueeze(1).to_broadcast([P, TILES, C]), ALU.max, ALU.mult)
                    dve.drain()
                    dve.tensor_reduce(logit[:, 0, :], zw[:, :, :], axis=AX.X, op=ALU.add).then_inc(s_bs, 1)
                    dve.wait_ge(s_bs, at + 6)
                    dve.tensor_tensor(ahot[:, 0, :, :], hot[:, 0, :, :],
                                      a[:, 0, :].unsqueeze(2).to_broadcast([P, TILES, WIN]), ALU.mult).then_inc(s_bs, 1)
                    dve.wait_ge(s_bs, at + 8)
                    row = nc.s_assert_within(node + v * WIN, 0, N - 1)
                    win = acc[:, bass.ds(row, WIN)]
                    dve.tensor_tensor(win, win, out_ps[:, 0, 0:WIN], ALU.add).then_inc(s_bs, 1)
                beyond(dve, l, window)
                dve.drain().then_inc(s_bi, 1)

                def window_pick(i, s, k):
                    dve.wait_ge(s_ld[k], (uses(l, i, k) + 1) * LOADS)
                    dve.wait_ge(s_zr, freed(l, s, SLOTS))
                    dve.tensor_scalar(left[k][0:PICK, :], rel[k][:, :], pidx[0:PICK, :], None, ALU.is_equal).then_inc(s_pick, 1)

                def z_sum(i, s, k):
                    dve.wait_ge(s_r, done(l, s))
                    dve.wait_ge(s_gat[k], (uses(l, i, k) + 1) * (16 * TILES))
                    dve.wait_ge(s_zw, freed(l, s, 1))
                    dve.tensor_tensor(z[:, :, :], z_part(k % 2), msg[k][:, :, 0:C], ALU.add).then_inc(s_zsum, 1)

                def edge_hot(i, s, k):
                    dve.wait_ge(s_ahot, freed(l, s, 2))
                    dve.tensor_tensor(hot[:, k % 2, :, :], iota_w[:, :].unsqueeze(1).to_broadcast([P, TILES, WIN]),
                                      rel_all[:, bass.ds(s * TILES, TILES)].unsqueeze(2).to_broadcast([P, TILES, WIN]),
                                      ALU.is_equal).then_inc(s_hot, 1)

                def z_weighted(i, s, k):
                    dve.wait_ge(s_zsum, done(l, s))
                    dve.wait_ge(s_log, freed(l, s, 1))
                    dve.scalar_tensor_tensor(zw[:, :, :], z[:, :, :], 0.0,
                                             wa2_c.unsqueeze(1).to_broadcast([P, TILES, C]),
                                             ALU.max, ALU.mult).then_inc(s_zw, 1)

                def logits(i, s, k):
                    dve.wait_ge(s_zw, done(l, s))
                    dve.wait_ge(s_a, freed(l, s, 2))
                    dve.tensor_reduce(logit[:, k % 2, :], zw[:, :, :], axis=AX.X, op=ALU.add).then_inc(s_log, 1)

                def hot_times_a(i, s, k):
                    dve.wait_ge(s_a, done(l, s))
                    dve.wait_ge(s_hot, done(l, s))
                    dve.wait_ge(s_sc, freed(l, s, 2))
                    dve.tensor_tensor(ahot[:, k % 2, :, :], hot[:, k % 2, :, :],
                                      a[:, k % 2, :].unsqueeze(2).to_broadcast([P, TILES, WIN]), ALU.mult).then_inc(s_ahot, 1)

                def add(i, s, k):
                    base = dve.value_load(base_i[0:1, bass.ds(s, 1)], min_val=0, max_val=N - 1)
                    dve.wait_ge(s_sc, done(l, s))
                    dve.wait_ge(s_acc, freed(l, s, 1))
                    win = acc[:, bass.ds(base, WIN)]
                    dve.tensor_tensor(win, win, out_ps[:, k % 2, 0:WIN], ALU.add).then_inc(s_acc, 1)

                gain = lambda t: t.unsqueeze(1).to_broadcast([P, LB, C])

                def centre(q, u, v, s):
                    dve.wait_ge(s_as, group_done(l, q))
                    dve.tensor_copy(acc_group(q), zeros[:, :]).then_inc(s_clear, 1)
                    dve.wait_ge(s_up, group_done(l, q))
                    dve.wait_ge(s_ub, (l * LGROUPS + q - u) * BSTEPS + 1)
                    n = (l * LGROUPS + q) * ASTEPS + 1
                    dve.wait_ge(s_ua, n)
                    dve.tensor_tensor(p1[:, u, :, :], update_bank(u)[:, 0:LB * C].rearrange("p (b c) -> p b c", c=C),
                                      gain(bias_c), ALU.add).then_inc(s_ua, 1)
                    dve.wait_ge(s_ua, n + 1)
                    squares(p1[:, u, :, :], p1[:, u, :, :], p2[:, u, :, :], pst[:, u, :, :], LB, s_ua, n + 1).then_inc(s_var, 1)

                def new_h(q, u, v, s):
                    n = (l * LGROUPS + q) * BSTEPS + 1
                    dve.wait_ge(s_root, group_done(l, q))
                    dve.reciprocal(pst[:, u, 3, :], pst[:, u, 2, :]).then_inc(s_ub, 1)
                    dve.wait_ge(s_ub, n + 1)
                    dve.tensor_tensor(p1[:, u, :, :], p2[:, u, :, :], pst[:, u, 3, :].unsqueeze(2).to_broadcast([P, LB, C]),
                                      ALU.mult).then_inc(s_ub, 1)
                    dve.wait_ge(s_ub, n + 2)
                    dve.tensor_tensor(p2[:, u, :, :], p1[:, u, :, :], gain(g_c), ALU.mult).then_inc(s_ub, 1)
                    dve.wait_ge(s_ub, n + 3)
                    dve.tensor_tensor(p1[:, u, :, :], p2[:, u, :, :], gain(b_c), ALU.add).then_inc(s_ub, 1)
                    dve.wait_ge(s_ub, n + 4)
                    dve.scalar_tensor_tensor(h_group(q), p1[:, u, :, :], floor_c, h_group(q), ALU.max, ALU.add).then_inc(s_ub, 1)

                def results(q, u, v, s):
                    with dve.If(l < L - 1):
                        n = (l * LGROUPS + q) * TSTEPS + 1
                        dve.wait_ge(s_ltp, group_done(l, q))
                        dve.wait_ge(s_lw[u], (l * TURNS[u] + v) * 16 + 16)
                        dve.wait_ge(s_lp[u], (l * TURNS[u] + v) * 16 + 16)
                        dve.wait_ge(s_lt, n)
                        dve.tensor_copy(tabs[:, u, 0:LB, :],
                                        update_bank(u)[:, LB * C:LB * 4 * C].rearrange("p (b f) -> p b f", b=LB)).then_inc(s_lt, 1)
                        p_parts(lambda t: pparts[:, u, 0:LB, t, :], tabs[:, u, 0:LB, 2 * C:3 * C], plow[:, 0:LB, :],
                                s_lt, n + 1)
                    dve.nop()
                    with dve.If(l > L - 2):
                        dve.wait_ge(s_ub, (l * LGROUPS + q + 1) * BSTEPS + 1)
                        dve.wait_ge(s_lw[u], (L - 1) * TURNS[u] * 16 + 16)
                        dve.wait_ge(s_out[u], v * 16 + 16)
                        dve.wait_ge(s_xg[u], v * 16 + (32 if isinstance(q, int) and q == LGROUPS - 1 else 16))
                        dve.tensor_tensor(tabs[:, u, 0:LB, 0:C], h_group(q), xg[:, u, :, :], ALU.add).then_inc(s_o, 1)
                    dve.nop()
                supertiles(dve, [(0, window_pick), (1, z_sum), (1, edge_hot), (1, z_weighted), (2, hot_times_a),
                                 (1, logits), (3, add)], [(4, centre), (6, new_h), (10, results)])


def latest(supertiles, nodes):
    behind = 1
    while any(supertiles * (q + 1) * LB * P / nodes + SLACK > STRIDE * (q + behind)
              for q in looped(supertiles, nodes, behind)):
        behind += 1
    return behind


def looped(supertiles, nodes, behind=None):
    behind = behind or latest(supertiles, nodes)
    strides = (supertiles - 1) // STRIDE
    return range(max(0, min(strides - behind, -(-nodes // (LB * P)) - 1)))


def first_node(supertiles, nodes):
    behind, count = latest(supertiles, nodes), len(looped(supertiles, nodes))
    taken = np.clip(np.arange(supertiles) // STRIDE - behind + 1, 0, count)
    return (taken * LB * P).astype(np.float32)


_WEIGHTS = ["W_node", "W_e1", "b_e1", "W_e2", "b_e2", "Wa1", "ba1", "Wa2", "ba2", "bias", "ln_g", "ln_b"]


def part_mask(attrs):
    part = [j for j in range(PARTS) for _ in range((PARTS - j) * attrs)] + list(range(PARTS))
    m = np.zeros((P, PARTS), np.float32)
    m[np.arange(PICK, PICK + len(part)), part] = 1.0
    return m


def laid_out(inputs):
    keep = np.ascontiguousarray
    src, dst = np.asarray(inputs["src"]), np.asarray(inputs["dst"])
    w = {k: keep(inputs["L0_gnn_" + k]) for k in _WEIGHTS}
    return {
        "x_dram": keep(inputs["x"]),
        "src_t_dram": keep(src.reshape(-1, P).T),
        "dst_t_dram": keep(dst.reshape(-1, P).T),
        "dst_dram": keep(dst),
        "eattr_t_dram": keep(np.asarray(inputs["edge_attr_3"]).T),
        "w_node_dram": w["W_node"],
        "w_node_t_dram": keep(w["W_node"].transpose(0, 2, 1)),
        "w_e1_dram": w["W_e1"], "b_e1_dram": w["b_e1"], "w_e2_dram": w["W_e2"], "b_e2_dram": w["b_e2"],
        "wa1_dram": w["Wa1"], "ba1_dram": w["ba1"], "wa2_dram": w["Wa2"], "ba2_dram": w["ba2"],
        "bias_dram": w["bias"], "ln_g_dram": w["ln_g"], "ln_b_dram": w["ln_b"],
        "ident_dram": np.eye(P, dtype=np.float32),
        "ones_dram": np.ones((1, GB * P), np.float32),
        "window_row_dram": (np.arange(P) // PARTS).astype(np.float32).reshape(P, 1),
        "part_mask_dram": part_mask(3),
        "ones_bf_dram": np.ones((PARTS, EDGES), mybir.dt.np(BF16)),
        "first_node_dram": first_node(dst.size // EDGES, inputs["x"].shape[0]),
    }


def kernel(**inputs):
    import concourse.bacc as _bacc
    from concourse.bass_utils import run_bass_kernel_spmd as _run

    arrays = laid_out(inputs)
    nc = _bacc.Bacc("TRN2", target_bir_lowering=False, num_devices=1)
    args = [nc.dram_tensor(k, a.shape, mybir.dt.from_np(a.dtype), kind="ExternalInput").ap() for k, a in arrays.items()]
    out = nc.dram_tensor("out_dram", arrays["x_dram"].shape, F32, kind="ExternalOutput").ap()
    gnn_kernel(nc, *args, out)
    return _run(nc, [arrays], core_ids=[0]).results[0]["out_dram"]
```
